# Optimizing a Trainium2 kernel written in Bass

```python
import numpy as np
import jax
import jax.numpy as jnp

def _softmax(x, axis=-1):
    return jax.nn.softmax(x, axis=axis)

def _gelu(x):
    return jax.nn.gelu(x, approximate=True)

def _silu(x):
    return jax.nn.silu(x)

def _sigmoid(x):
    return jax.nn.sigmoid(x)

def _layernorm(x, axis=-1, eps=1e-05):
    m = jnp.mean(x, axis=axis, keepdims=True)
    v = jnp.var(x, axis=axis, keepdims=True)
    return (x - m) / jnp.sqrt(v + eps)

def _scatter_add(tgt, idx, src, axis=0):
    return tgt.at[idx].add(src)

def _segment_sum(src, seg, n):
    return jax.ops.segment_sum(src, seg, n)
kernel_name = 'mk_dlrm_tower_d1_rec_r8_a58824'

def setup_inputs(seed: int=0):
    np.random.seed(seed)
    _w = jnp.asarray

    def _rec_inputs():
        import jax
        import jax.numpy as jnp
        _tk = jax.random.key(seed)
        dense_ctx = jax.random.normal(jax.random.fold_in(_tk, 190), (1024, 16), jnp.float32)
        ids = jnp.stack([jax.random.randint(jax.random.fold_in(_tk, 200 + f), (1024,), 0, v, jnp.int32) for f, v in enumerate([1000, 1250, 1250, 1250, 12500, 125000, 125000, 125000, 1000, 12500, 1000, 1250, 12500, 1250, 1250, 12500, 1250, 1000, 1000, 1250, 1250, 12500, 12500, 1250, 1250, 1000, 1250, 1250, 12500, 1000, 1250, 1000, 1250, 1250, 1000, 1250, 1250, 1250, 1000, 1000])], axis=1)
        tbl_0 = 0.05 * jax.random.normal(jax.random.fold_in(_tk, 500 + 0), (1000, 64), jnp.float32)
        tbl_1 = 0.05 * jax.random.normal(jax.random.fold_in(_tk, 500 + 1), (1250, 64), jnp.float32)
        tbl_2 = 0.05 * jax.random.normal(jax.random.fold_in(_tk, 500 + 2), (1250, 64), jnp.float32)
        tbl_3 = 0.05 * jax.random.normal(jax.random.fold_in(_tk, 500 + 3), (1250, 64), jnp.float32)
        tbl_4 = 0.05 * jax.random.normal(jax.random.fold_in(_tk, 500 + 4), (12500, 64), jnp.float32)
        tbl_5 = 0.05 * jax.random.normal(jax.random.fold_in(_tk, 500 + 5), (125000, 64), jnp.float32)
        tbl_6 = 0.05 * jax.random.normal(jax.random.fold_in(_tk, 500 + 6), (125000, 64), jnp.float32)
        tbl_7 = 0.05 * jax.random.normal(jax.random.fold_in(_tk, 500 + 7), (125000, 64), jnp.float32)
        tbl_8 = 0.05 * jax.random.normal(jax.random.fold_in(_tk, 500 + 8), (1000, 64), jnp.float32)
        tbl_9 = 0.05 * jax.random.normal(jax.random.fold_in(_tk, 500 + 9), (12500, 64), jnp.float32)
        tbl_10 = 0.05 * jax.random.normal(jax.random.fold_in(_tk, 500 + 10), (1000, 64), jnp.float32)
        tbl_11 = 0.05 * jax.random.normal(jax.random.fold_in(_tk, 500 + 11), (1250, 64), jnp.float32)
        tbl_12 = 0.05 * jax.random.normal(jax.random.fold_in(_tk, 500 + 12), (12500, 64), jnp.float32)
        tbl_13 = 0.05 * jax.random.normal(jax.random.fold_in(_tk, 500 + 13), (1250, 64), jnp.float32)
        tbl_14 = 0.05 * jax.random.normal(jax.random.fold_in(_tk, 500 + 14), (1250, 64), jnp.float32)
        tbl_15 = 0.05 * jax.random.normal(jax.random.fold_in(_tk, 500 + 15), (12500, 64), jnp.float32)
        tbl_16 = 0.05 * jax.random.normal(jax.random.fold_in(_tk, 500 + 16), (1250, 64), jnp.float32)
        tbl_17 = 0.05 * jax.random.normal(jax.random.fold_in(_tk, 500 + 17), (1000, 64), jnp.float32)
        tbl_18 = 0.05 * jax.random.normal(jax.random.fold_in(_tk, 500 + 18), (1000, 64), jnp.float32)
        tbl_19 = 0.05 * jax.random.normal(jax.random.fold_in(_tk, 500 + 19), (1250, 64), jnp.float32)
        tbl_20 = 0.05 * jax.random.normal(jax.random.fold_in(_tk, 500 + 20), (1250, 64), jnp.float32)
        tbl_21 = 0.05 * jax.random.normal(jax.random.fold_in(_tk, 500 + 21), (12500, 64), jnp.float32)
        tbl_22 = 0.05 * jax.random.normal(jax.random.fold_in(_tk, 500 + 22), (12500, 64), jnp.float32)
        tbl_23 = 0.05 * jax.random.normal(jax.random.fold_in(_tk, 500 + 23), (1250, 64), jnp.float32)
        tbl_24 = 0.05 * jax.random.normal(jax.random.fold_in(_tk, 500 + 24), (1250, 64), jnp.float32)
        tbl_25 = 0.05 * jax.random.normal(jax.random.fold_in(_tk, 500 + 25), (1000, 64), jnp.float32)
        tbl_26 = 0.05 * jax.random.normal(jax.random.fold_in(_tk, 500 + 26), (1250, 64), jnp.float32)
        tbl_27 = 0.05 * jax.random.normal(jax.random.fold_in(_tk, 500 + 27), (1250, 64), jnp.float32)
        tbl_28 = 0.05 * jax.random.normal(jax.random.fold_in(_tk, 500 + 28), (12500, 64), jnp.float32)
        tbl_29 = 0.05 * jax.random.normal(jax.random.fold_in(_tk, 500 + 29), (1000, 64), jnp.float32)
        tbl_30 = 0.05 * jax.random.normal(jax.random.fold_in(_tk, 500 + 30), (1250, 64), jnp.float32)
        tbl_31 = 0.05 * jax.random.normal(jax.random.fold_in(_tk, 500 + 31), (1000, 64), jnp.float32)
        tbl_32 = 0.05 * jax.random.normal(jax.random.fold_in(_tk, 500 + 32), (1250, 64), jnp.float32)
        tbl_33 = 0.05 * jax.random.normal(jax.random.fold_in(_tk, 500 + 33), (1250, 64), jnp.float32)
        tbl_34 = 0.05 * jax.random.normal(jax.random.fold_in(_tk, 500 + 34), (1000, 64), jnp.float32)
        tbl_35 = 0.05 * jax.random.normal(jax.random.fold_in(_tk, 500 + 35), (1250, 64), jnp.float32)
        tbl_36 = 0.05 * jax.random.normal(jax.random.fold_in(_tk, 500 + 36), (1250, 64), jnp.float32)
        tbl_37 = 0.05 * jax.random.normal(jax.random.fold_in(_tk, 500 + 37), (1250, 64), jnp.float32)
        tbl_38 = 0.05 * jax.random.normal(jax.random.fold_in(_tk, 500 + 38), (1000, 64), jnp.float32)
        tbl_39 = 0.05 * jax.random.normal(jax.random.fold_in(_tk, 500 + 39), (1000, 64), jnp.float32)
        _rk = jax.random.fold_in(_tk, 7)
        W_top1 = 0.0354441 * jax.random.normal(jax.random.fold_in(_tk, 801), (796, 512), jnp.float32)
        W_top2 = 0.0441942 * jax.random.normal(jax.random.fold_in(_tk, 802), (512, 256), jnp.float32)
        W_top3 = 0.0625 * jax.random.normal(jax.random.fold_in(_tk, 803), (256, 1), jnp.float32)
        b_top1 = jnp.zeros((512,), jnp.float32)
        b_top2 = jnp.zeros((256,), jnp.float32)
        return (dense_ctx, ids, tbl_0, tbl_1, tbl_2, tbl_3, tbl_4, tbl_5, tbl_6, tbl_7, tbl_8, tbl_9, tbl_10, tbl_11, tbl_12, tbl_13, tbl_14, tbl_15, tbl_16, tbl_17, tbl_18, tbl_19, tbl_20, tbl_21, tbl_22, tbl_23, tbl_24, tbl_25, tbl_26, tbl_27, tbl_28, tbl_29, tbl_30, tbl_31, tbl_32, tbl_33, tbl_34, tbl_35, tbl_36, tbl_37, tbl_38, tbl_39, W_top1, b_top1, W_top2, b_top2, W_top3)
    dense_ctx, ids, tbl_0, tbl_1, tbl_2, tbl_3, tbl_4, tbl_5, tbl_6, tbl_7, tbl_8, tbl_9, tbl_10, tbl_11, tbl_12, tbl_13, tbl_14, tbl_15, tbl_16, tbl_17, tbl_18, tbl_19, tbl_20, tbl_21, tbl_22, tbl_23, tbl_24, tbl_25, tbl_26, tbl_27, tbl_28, tbl_29, tbl_30, tbl_31, tbl_32, tbl_33, tbl_34, tbl_35, tbl_36, tbl_37, tbl_38, tbl_39, W_top1, b_top1, W_top2, b_top2, W_top3 = _rec_inputs()

    def _L0_rec_setup():
        import jax, jax.numpy as jnp
        import numpy as np

        def _pair_indices(num_fields):
            i_idx, j_idx = np.triu_indices(num_fields, k=1)
            return (jnp.asarray(i_idx), jnp.asarray(j_idx))
        key = jax.random.key(seed)
        k1, k2 = jax.random.split(key)
        B, F, D = (256, 40, 64)
        P = F * (F - 1) // 2
        x = jax.random.normal(k1, (B, F, D), dtype=jnp.float32)
        W = jax.random.normal(k2, (P, D, D), dtype=jnp.float32) * (1.0 / np.sqrt(D))
        return {'x': x, 'W': W}
    _L0_rec_all = _L0_rec_setup()
    _L0_rec_in = {k: v for k, v in _L0_rec_all.items() if k in ('W',)}
    del _L0_rec_all
    return {'dense_ctx': dense_ctx, 'ids': ids, 'tbl_0': tbl_0, 'tbl_1': tbl_1, 'tbl_2': tbl_2, 'tbl_3': tbl_3, 'tbl_4': tbl_4, 'tbl_5': tbl_5, 'tbl_6': tbl_6, 'tbl_7': tbl_7, 'tbl_8': tbl_8, 'tbl_9': tbl_9, 'tbl_10': tbl_10, 'tbl_11': tbl_11, 'tbl_12': tbl_12, 'tbl_13': tbl_13, 'tbl_14': tbl_14, 'tbl_15': tbl_15, 'tbl_16': tbl_16, 'tbl_17': tbl_17, 'tbl_18': tbl_18, 'tbl_19': tbl_19, 'tbl_20': tbl_20, 'tbl_21': tbl_21, 'tbl_22': tbl_22, 'tbl_23': tbl_23, 'tbl_24': tbl_24, 'tbl_25': tbl_25, 'tbl_26': tbl_26, 'tbl_27': tbl_27, 'tbl_28': tbl_28, 'tbl_29': tbl_29, 'tbl_30': tbl_30, 'tbl_31': tbl_31, 'tbl_32': tbl_32, 'tbl_33': tbl_33, 'tbl_34': tbl_34, 'tbl_35': tbl_35, 'tbl_36': tbl_36, 'tbl_37': tbl_37, 'tbl_38': tbl_38, 'tbl_39': tbl_39, 'W_top1': W_top1, 'b_top1': b_top1, 'W_top2': W_top2, 'b_top2': b_top2, 'W_top3': W_top3, 'L0_rec_W': _L0_rec_in['W']}

def reference(dense_ctx, ids, tbl_0, tbl_1, tbl_2, tbl_3, tbl_4, tbl_5, tbl_6, tbl_7, tbl_8, tbl_9, tbl_10, tbl_11, tbl_12, tbl_13, tbl_14, tbl_15, tbl_16, tbl_17, tbl_18, tbl_19, tbl_20, tbl_21, tbl_22, tbl_23, tbl_24, tbl_25, tbl_26, tbl_27, tbl_28, tbl_29, tbl_30, tbl_31, tbl_32, tbl_33, tbl_34, tbl_35, tbl_36, tbl_37, tbl_38, tbl_39, W_top1, b_top1, W_top2, b_top2, W_top3, L0_rec_W):
    import jax
    import jax.numpy as jnp

    def _L0_rec_ref(x, W):
        import jax, jax.numpy as jnp
        import numpy as np

        def _pair_indices(num_fields):
            i_idx, j_idx = np.triu_indices(num_fields, k=1)
            return (jnp.asarray(i_idx), jnp.asarray(j_idx))
        B, F, D = x.shape
        i_idx, j_idx = _pair_indices(F)
        vi = x[:, i_idx, :]
        vj = x[:, j_idx, :]
        viW = jnp.einsum('bpd,pde->bpe', vi, W)
        out = jnp.einsum('bpe,bpe->bp', viW, vj)
        return out
    e = jnp.stack([tbl_0[ids[:, 0]], tbl_1[ids[:, 1]], tbl_2[ids[:, 2]], tbl_3[ids[:, 3]], tbl_4[ids[:, 4]], tbl_5[ids[:, 5]], tbl_6[ids[:, 6]], tbl_7[ids[:, 7]], tbl_8[ids[:, 8]], tbl_9[ids[:, 9]], tbl_10[ids[:, 10]], tbl_11[ids[:, 11]], tbl_12[ids[:, 12]], tbl_13[ids[:, 13]], tbl_14[ids[:, 14]], tbl_15[ids[:, 15]], tbl_16[ids[:, 16]], tbl_17[ids[:, 17]], tbl_18[ids[:, 18]], tbl_19[ids[:, 19]], tbl_20[ids[:, 20]], tbl_21[ids[:, 21]], tbl_22[ids[:, 22]], tbl_23[ids[:, 23]], tbl_24[ids[:, 24]], tbl_25[ids[:, 25]], tbl_26[ids[:, 26]], tbl_27[ids[:, 27]], tbl_28[ids[:, 28]], tbl_29[ids[:, 29]], tbl_30[ids[:, 30]], tbl_31[ids[:, 31]], tbl_32[ids[:, 32]], tbl_33[ids[:, 33]], tbl_34[ids[:, 34]], tbl_35[ids[:, 35]], tbl_36[ids[:, 36]], tbl_37[ids[:, 37]], tbl_38[ids[:, 38]], tbl_39[ids[:, 39]]], axis=1)
    z = _L0_rec_ref(e, L0_rec_W)
    z = z.reshape(z.shape[0], -1)
    h = jnp.concatenate([z, dense_ctx], axis=1)
    h = jnp.maximum(h @ W_top1 + b_top1, 0.0)
    h = jnp.maximum(h @ W_top2 + b_top2, 0.0)
    y = h @ W_top3
    return y

_drawn_inputs = setup_inputs


def setup_inputs(seed=0):
    import zlib

    import numpy as np

    out = dict(_drawn_inputs(seed))
    spreads = {'b_top1': (0.0, 0.1), 'b_top2': (0.0, 0.1)}
    factors = {'tbl_0': 2.73}
    for name, (base, spread) in spreads.items():
        noise = np.random.default_rng([zlib.crc32(name.encode()), seed]).standard_normal(out[name].shape)
        drawn = base * np.exp(spread * noise) if base else spread * noise
        out[name] = jnp.asarray(drawn.astype(out[name].dtype))
    for name, factor in factors.items():
        out[name] = (out[name] * factor).astype(out[name].dtype)
    return out
```

```python
from contextlib import ExitStack

import concourse.bass as bass
from concourse import mybir

F32 = mybir.dt.float32
F32R = mybir.dt.float32r
I32 = mybir.dt.int32
ALU = mybir.AluOpType
ACT = mybir.ActivationFunctionType
AX = mybir.AxisListType

P = 128
BANK = 512
UNIT_BANKS = 3
PIECE_PAIRS = 20
RAW_SLOTS = 3
PRODUCT_SLOTS = 6
TWIN_SLOTS = 2
OCTANT = 8
GATHER_AHEAD = 2


class Unit:

    def __init__(self, m, tile, tiles, i0, i1):
        self.m, self.tile, self.tiles, self.i0, self.i1 = m, tile, tiles, i0, i1
        self.pairs = tiles * (i1 - i0)
        self.how = "vector"


def plan(F, D, NB):
    per_bank = BANK // D
    units, pieces, of_stage = [], [], {}
    for m in range(1, F):
        first = len(units)
        if m <= per_bank:
            for t in range(0, NB, UNIT_BANKS):
                units.append(Unit(m, t, min(UNIT_BANKS, NB - t), 0, m))
        else:
            cuts = [0, m] if m <= UNIT_BANKS * per_bank else [0, (m + 1) // 2, m]
            for t in range(NB):
                for a, b in zip(cuts, cuts[1:]):
                    units.append(Unit(m, t, 1, a, b))
        of_stage[m] = range(first, len(units))
        for a in range(0, m, PIECE_PAIRS):
            pieces.append((m, a, min(a + PIECE_PAIRS, m)))

    vec = ten = sca = gps = 0.0
    for m in range(1, F):
        gps += NB * 1040.0
        sca += m * D * 0.85 + NB * P * 0.85 + 400
        vec += 2 * m * D / 0.96 * 0.5 + NB * P / 0.96 + 250
        ready = (m + 1) * NB * 1040.0
        vec, sca, ten = max(vec, ready), max(sca, ready), max(ten, ready)
        gps = max(gps, ready)
        for u in of_stage[m]:
            n, unit = units[u].pairs * D, units[u]
            vec += n / 0.96 + 70
            ten += n * 0.84 + 60
            done = {"vector": vec + n / 0.96 + 70}
            if unit.tiles == 1 and unit.pairs >= 9:
                done["tensor"] = max(ten + n * 1.667 + 200, vec + n / OCTANT / 0.96 + 70)
                done["scalar"] = max(sca + 240 * unit.pairs, vec)
                done["gpsimd"] = max(gps + n * 1.17, vec + n / 2 / 0.96 + 70)
            unit.how = min(done, key=done.get)
            if unit.how == "vector":
                vec += n / 0.96 + 70
            elif unit.how == "tensor":
                ten, vec = ten + n * 1.667 + 200, vec + n / OCTANT / 0.96 + 70
            elif unit.how == "scalar":
                sca += 240 * unit.pairs
            else:
                gps, vec = gps + n * 1.17, vec + n / 2 / 0.96 + 70

    sum_lag = {"vector": 0, "scalar": 0, "gpsimd": 0, "tensor": 2}
    finish_lag = {"vector": 1, "gpsimd": 4, "tensor": 3}
    after = {u: [] for u in range(len(units))}
    steps = [("gather", m) for m in range(GATHER_AHEAD)]

    def prepare(m):
        w = [q for q, piece in enumerate(pieces) if piece[0] == m]
        out = [("transpose", m, 0)] + [("w_high", q) for q in w[:1]] + [("x_high", m, 0)]
        out += [("w_low", q) for q in w[:1]] + [("x_low", m, 0)]
        out += [("transpose", m, 1)] + [("w_high", q) for q in w[1:]] + [("x_high", m, 1)]
        return out + [("w_low", q) for q in w[1:]] + [("x_low", m, 1)]

    steps += prepare(1)
    for m in range(1, F - 1):
        span = of_stage[m]
        todo = prepare(m + 1)
        for k, step in enumerate(todo):
            after[span[min(k * len(span) // len(todo), len(span) - 1)]].append(step)
    last = len(units) - 1
    tail = []
    for u, unit in enumerate(units):
        if unit.how != "scalar":
            at = u + finish_lag[unit.how]
            (after[at] if at < last else tail).append(("finish", u))
    for u, unit in enumerate(units):
        if unit.how != "vector":
            at = u + sum_lag[unit.how]
            (after[at] if at < last else tail).append(("sum", u))
    tail.sort(key=lambda step: (step[1], step[0] == "finish"))
    for m in range(1, F):
        if m + GATHER_AHEAD - 1 < F:
            steps.append(("gather", m + GATHER_AHEAD - 1))
        for u in of_stage[m]:
            steps.append(("unit", u))
            steps += after[u]
    return units, pieces, steps + tail, of_stage


def build(nc, tables, ids, dense, weights, eye, w1, b1, w2, b2, w3, out):
    B, F = ids.shape
    D = tables[0].shape[1]
    NB = B // P
    HALF = BANK // P
    PAIRS = F * (F - 1) // 2
    H1, H2 = w2.shape
    K1 = w1.shape[0]
    KT = -(-K1 // P)
    N1, N2 = H1 // P, H2 // P
    units, pieces, steps, of_stage = plan(F, D, NB)
    base = [m * (m - 1) // 2 for m in range(F + 1)]

    with ExitStack() as ctx:
        def sb(name, shape, dt=F32):
            return ctx.enter_context(nc.sbuf_tensor(name, shape, dt))

        def ps(name, shape):
            return ctx.enter_context(nc.psum_tensor(name, shape, F32))

        def sem(name):
            return ctx.enter_context(nc.semaphore(name))

        idx = sb("idx", [P, NB, F], I32)
        emb = sb("emb", [P, NB, F * D])
        ident = sb("ident", [P, P])
        raw = sb("raw", [P, RAW_SLOTS, PIECE_PAIRS * D])
        wsplit = sb("wsplit", [P, 2, (F - 1) * D], F32R)
        xsplit = sb("xsplit", [P, 2, 2, NB * P], F32R)
        twin = sb("twin", [P, TWIN_SLOTS, NB, 2, D])
        prod = sb("prod", [P, PRODUCT_SLOTS, UNIT_BANKS * BANK])
        z = sb("z", [P, NB, K1])
        w2_sb = sb("w2_sb", [P, N1, H2])
        w3_sb = sb("w3_sb", [P, N2])
        b1_sb = sb("b1_sb", [P, N1])
        b2_sb = sb("b2_sb", [P, N2])
        emb_flat = emb[:, :, :].rearrange("p t c -> p (t c)")
        zt = emb_flat[:, 0:KT * B].rearrange("p (k b) -> p k b", k=KT)
        h1t = emb_flat[:, KT * B:(KT + N1) * B].rearrange("p (k b) -> p k b", k=N1)
        h2t = emb_flat[:, (KT + N1) * B:(KT + N1 + N2) * B].rearrange("p (k b) -> p k b", k=N2)
        y_sb = emb_flat[0:1, (KT + N1 + N2) * B:(KT + N1 + N2 + 1) * B]
        raw_flat = raw[:, :, :].rearrange("p s c -> p (s c)")
        w1_sb = raw_flat[:, 0:KT * H1].rearrange("p (k n) -> p k n", k=KT)

        uacc = ps("uacc", [P, 2, UNIT_BANKS, BANK])
        tbank = ps("tbank", [P, BANK])
        fold = ps("fold", [P, BANK])

        idx_loaded = sem("idx_loaded")
        ident_loaded = sem("ident_loaded")
        dense_loaded = sem("dense_loaded")
        mlp_loaded = sem("mlp_loaded")
        gathered = [sem(f"gathered{m}") for m in range(F)]
        raw_loaded = [sem(f"raw_loaded{s}") for s in range(RAW_SLOTS)]
        twin_copied = [sem(f"twin_copied{s}") for s in range(TWIN_SLOTS)]
        w_high_done = sem("w_high_done")
        w_low_done = sem("w_low_done")
        x_transposed = sem("x_transposed")
        x_high_done = sem("x_high_done")
        x_low_done = sem("x_low_done")
        u_ready = sem("u_ready")
        prod_ready = sem("prod_ready")
        halved = sem("halved")
        folded = sem("folded")
        z_by_vector = sem("z_by_vector")
        z_by_scalar = sem("z_by_scalar")
        mlp_acc = sem("mlp_acc")
        mlp_by_scalar = sem("mlp_by_scalar")
        mlp_by_vector = sem("mlp_by_vector")
        out_stored = sem("out_stored")

        sum_count, finish_count, counts = {}, {}, {"scalar": 0, "gpsimd": 0, "tensor": 0}
        for step in steps:
            if step[0] == "sum":
                how = units[step[1]].how
                counts[how] += 1
                sum_count[step[1]] = counts[how]
            elif step[0] == "finish":
                finish_count[step[1]] = len(finish_count) + 1
        last_piece = {m: max(q for q, pc in enumerate(pieces) if pc[0] == m) for m in range(1, F)}

        def cols(n):
            return slice(n * P, (n + 1) * P)

        def z_of(unit):
            c = base[unit.m] + unit.i0
            return z[:, unit.tile:unit.tile + unit.tiles, c:c + unit.i1 - unit.i0]

        def product_of(u):
            return prod[:, u % PRODUCT_SLOTS, 0:units[u].pairs * D]

        mlp = [("zt", k, h) for h in range(2) for k in range(KT)]
        mlp += [("h1", n, h) for h in range(2) for n in range(N1)]
        mlp += [("h2", n, h) for h in range(2) for n in range(N2)]
        mlp += [("y", 0, h) for h in range(2)]
        mlp_banks = [uacc[:, s, c, :] for s in range(2) for c in range(UNIT_BANKS)] + [tbank[:, :], fold[:, :]]

        def mlp_bank(t):
            return mlp_banks[t % len(mlp_banks)]

        def wait_mlp_task(eng, t):
            eng.wait_ge(mlp_by_vector if t % 2 else mlp_by_scalar, t // 2 + 1)

        block = ctx.enter_context(nc.Block())

        @block.sync
        def _(sp):
            def copy_twin(m):
                sp.wait_ge(gathered[m], 16 * NB)
                if m > TWIN_SLOTS:
                    sp.wait_ge(x_transposed, 2 * (m - TWIN_SLOTS))
                for k in range(2):
                    sp.dma_start(twin[:, m % TWIN_SLOTS, :, k, :], emb[:, :, m * D:(m + 1) * D]
                                 ).then_inc(twin_copied[m % TWIN_SLOTS], 16)

            sp.dma_start(idx[:, :, :], ids.rearrange("(t p) f -> p t f", p=P)).then_inc(idx_loaded, 16)
            sp.dma_start(ident[:, :], eye).then_inc(ident_loaded, 16)
            for q, (m, a, b) in enumerate(pieces):
                if a == 0 and m > 1:
                    copy_twin(m - 1)
                if q >= RAW_SLOTS:
                    sp.wait_ge(w_low_done, q - RAW_SLOTS + 1)
                for half in range(2):
                    sp.dma_start(raw[half * D:(half + 1) * D, q % RAW_SLOTS, 0:(b - a) * D],
                                 weights[:, (base[m] + a) * D:(base[m] + b) * D]
                                 ).then_inc(raw_loaded[q % RAW_SLOTS], 16)
                if q == 0:
                    sp.dma_start(z[:, :, PAIRS:K1], dense.rearrange("(t p) f -> p t f", p=P)
                                 ).then_inc(dense_loaded, 16)
                    sp.dma_start(w2_sb[:, :, :], w2.rearrange("(k p) n -> p k n", p=P)).then_inc(mlp_loaded, 16)
                    sp.dma_start(w3_sb[:, :], w3).then_inc(mlp_loaded, 16)
                    sp.dma_start(b1_sb[:, :], b1).then_inc(mlp_loaded, 16)
                    sp.dma_start(b2_sb[:, :], b2).then_inc(mlp_loaded, 16)
            copy_twin(F - 1)
            sp.wait_ge(w_low_done, len(pieces))
            full = K1 // P
            sp.dma_start(w1_sb[:, 0:full, :], w1[0:full * P, :].rearrange("(k p) n -> p k n", p=P)
                         ).then_inc(mlp_loaded, 16)
            sp.dma_start(w1_sb[0:K1 - full * P, full, :], w1[full * P:K1, :]).then_inc(mlp_loaded, 16)
            wait_mlp_task(sp, len(mlp) - 2)
            wait_mlp_task(sp, len(mlp) - 1)
            sp.dma_start(out.rearrange("b o -> o b"), y_sb).then_inc(out_stored, 16)
            sp.wait_ge(out_stored, 16)

        @block.gpsimd
        def _(pool):
            pool.wait_ge(idx_loaded, 16)
            for kind, n, *_ in steps:
                if kind == "gather":
                    for t in range(NB):
                        pool.indirect_dma_start(
                            emb[:, t, n * D:(n + 1) * D], None, tables[n][:, :],
                            bass.IndirectOffsetOnAxis(ap=idx[:, t, n:n + 1], axis=0)).then_inc(gathered[n], 16)
                elif kind == "sum" and units[n].how == "gpsimd":
                    v = product_of(n).rearrange("p (j d) -> p j d", d=D)
                    pool.wait_ge(prod_ready, n + 1)
                    pool.tensor_tensor(v[:, :, 0:D // 2], v[:, :, 0:D // 2], v[:, :, D // 2:D],
                                       ALU.add).then_inc(halved, 1)

        @block.scalar
        def _(act):
            x_count = 0
            for kind, n, *rest in steps:
                if kind == "w_high":
                    m, a, b = pieces[n]
                    act.wait_ge(raw_loaded[n % RAW_SLOTS], 32 * (n // RAW_SLOTS + 1))
                    if m > 2:
                        act.wait_ge(u_ready, of_stage[m - 2][-1] + 1)
                        act.wait_ge(w_low_done, last_piece[m - 2] + 1)
                    act.activation(wsplit[:, m % 2, a * D:b * D], raw[:, n % RAW_SLOTS, 0:(b - a) * D],
                                   ACT.Copy).then_inc(w_high_done, 1)
                elif kind == "x_high":
                    h = rest[0]
                    x_count += 1
                    act.wait_ge(x_transposed, x_count)
                    if n > 2:
                        act.wait_ge(u_ready, of_stage[n - 2][-1] + 1)
                    act.activation(xsplit[:, n % 2, 0, h * BANK:(h + 1) * BANK], tbank[:, :],
                                   ACT.Copy).then_inc(x_high_done, 1)
                elif kind == "sum" and units[n].how == "scalar":
                    unit = units[n]
                    act.wait_ge(prod_ready, n + 1)
                    zv, pv = z_of(unit), product_of(n)
                    for j in range(unit.pairs):
                        last = act.activation(pv[:, j * D:(j + 1) * D], pv[:, j * D:(j + 1) * D], ACT.Copy,
                                              accum_out=zv[:, 0, j:j + 1])
                    last.then_inc(z_by_scalar, 1)
            act.wait_ge(mlp_loaded, 6 * 16)
            for t, (kind, n, h) in enumerate(mlp):
                if t % 2 == 0:
                    act.wait_ge(mlp_acc, t + 1)
                    rows = min(P, K1 - n * P)
                    half = slice(h * BANK, (h + 1) * BANK)
                    if kind == "zt":
                        ins = act.activation(zt[0:rows, n, half], mlp_bank(t)[0:rows, :], ACT.Copy)
                    elif kind == "h1":
                        ins = act.activation(h1t[:, n, half], mlp_bank(t), ACT.Relu, bias=b1_sb[:, n:n + 1])
                    elif kind == "h2":
                        ins = act.activation(h2t[:, n, half], mlp_bank(t), ACT.Relu, bias=b2_sb[:, n:n + 1])
                    else:
                        ins = act.activation(y_sb[0:1, half], mlp_bank(t)[0:1, :], ACT.Copy)
                    ins.then_inc(mlp_by_scalar, 1)

        @block.vector
        def _(dve):
            x_count = w_count = 0
            seen = 0
            for kind, n, *rest in steps:
                if kind == "w_low":
                    m, a, b = pieces[n]
                    w_count += 1
                    dve.wait_ge(w_high_done, w_count)
                    w = wsplit[D:2 * D, m % 2, a * D:b * D]
                    dve.tensor_tensor(w, raw[D:2 * D, n % RAW_SLOTS, 0:(b - a) * D], w.bitcast(F32),
                                      ALU.subtract).then_inc(w_low_done, 1)
                elif kind == "x_low":
                    half = slice(rest[0] * BANK, (rest[0] + 1) * BANK)
                    x_count += 1
                    dve.wait_ge(x_high_done, x_count)
                    dve.tensor_tensor(xsplit[:, n % 2, 1, half], tbank[:, :],
                                      xsplit[:, n % 2, 0, half].bitcast(F32), ALU.subtract).then_inc(x_low_done, 1)
                elif kind == "unit":
                    unit = units[n]
                    while seen < unit.m:
                        dve.wait_ge(gathered[seen], 16 * NB)
                        seen += 1
                    dve.wait_ge(u_ready, n + 1)
                    if n >= PRODUCT_SLOTS:
                        u = n - PRODUCT_SLOTS
                        how = units[u].how
                        if how == "scalar":
                            dve.wait_ge(z_by_scalar, sum_count[u])
                        else:
                            dve.wait_ge(z_by_vector, finish_count[u])
                    width = (unit.i1 - unit.i0) * D
                    e = emb[:, unit.tile:unit.tile + unit.tiles, unit.i0 * D:unit.i1 * D]
                    if unit.tiles == 1:
                        u_in = uacc[:, n % 2, :, :].rearrange("p c n -> p (c n)")[:, 0:width]
                        dve.tensor_tensor(product_of(n), u_in, e[:, 0, :], ALU.mult).then_inc(prod_ready, 1)
                    else:
                        dve.tensor_tensor(product_of(n).rearrange("p (t c) -> p t c", t=unit.tiles),
                                          uacc[:, n % 2, 0:unit.tiles, 0:width], e,
                                          ALU.mult).then_inc(prod_ready, 1)
                elif kind == "finish":
                    unit = units[n]
                    if unit.how == "tensor":
                        dve.wait_ge(folded, sum_count[n])
                        v = fold[:, 0:unit.pairs * OCTANT].rearrange("p (t j d) -> p t j d", t=unit.tiles, d=OCTANT)
                    else:
                        v = product_of(n).rearrange("p (t j d) -> p t j d", t=unit.tiles, d=D)
                        if unit.how == "gpsimd":
                            dve.wait_ge(halved, sum_count[n])
                            v = v[:, :, :, 0:D // 2]
                        else:
                            dve.wait_ge(prod_ready, n + 1)
                    dve.tensor_reduce(z_of(unit), v, AX.X, ALU.add).then_inc(z_by_vector, 1)
            dve.wait_ge(mlp_loaded, 6 * 16)
            for t, (kind, n, h) in enumerate(mlp):
                if t % 2 == 1:
                    dve.wait_ge(mlp_acc, t + 1)
                    rows = min(P, K1 - n * P)
                    half = slice(h * BANK, (h + 1) * BANK)
                    if kind == "zt":
                        ins = dve.tensor_copy(zt[0:rows, n, half], mlp_bank(t)[0:rows, :])
                    elif kind == "h1":
                        ins = dve.tensor_scalar(h1t[:, n, half], mlp_bank(t), b1_sb[:, n:n + 1], 0.0, ALU.add, ALU.max)
                    elif kind == "h2":
                        ins = dve.tensor_scalar(h2t[:, n, half], mlp_bank(t), b2_sb[:, n:n + 1], 0.0, ALU.add, ALU.max)
                    else:
                        ins = dve.tensor_copy(y_sb[0:1, half], mlp_bank(t)[0:1, :])
                    ins.then_inc(mlp_by_vector, 1)

        @block.tensor
        def _(pe):
            pe.wait_ge(ident_loaded, 16)
            x_count = 0
            for kind, n, *rest in steps:
                if kind == "transpose":
                    if rest[0] == 0:
                        slot = n % TWIN_SLOTS
                        pe.wait_ge(twin_copied[slot], 32 * ((n - (slot or TWIN_SLOTS)) // TWIN_SLOTS + 1))
                    if x_count:
                        pe.wait_ge(x_low_done, x_count)
                    x_count += 1
                    for t in range(HALF):
                        x = twin[:, n % TWIN_SLOTS, rest[0] * HALF + t, :, :].rearrange("p k d -> p (k d)")
                        last = pe.transpose(tbank[:, cols(t)], x, ident[:, :])
                    last.then_inc(x_transposed, 1)
                elif kind == "unit":
                    unit = units[n]
                    if n == of_stage[unit.m][0]:
                        pe.wait_ge(w_low_done, last_piece[unit.m] + 1)
                        pe.wait_ge(x_low_done, 2 * unit.m)
                    if n >= 2:
                        pe.wait_ge(prod_ready, n - 1)
                    width = (unit.i1 - unit.i0) * D
                    for t in range(unit.tiles):
                        for part in range(2):
                            for c in range(0, width, BANK):
                                w = min(BANK, width - c)
                                last = pe.matmul(uacc[:, n % 2, t + c // BANK, 0:w],
                                                 xsplit[:, unit.m % 2, part, cols(unit.tile + t)],
                                                 wsplit[:, unit.m % 2, unit.i0 * D + c:unit.i0 * D + c + w],
                                                 start=(part == 0), stop=(part == 1))
                    last.then_inc(u_ready, 1)
                elif kind == "sum" and units[n].how == "tensor":
                    pe.wait_ge(prod_ready, n + 1)
                    prev = [u for u in sum_count if units[u].how == "tensor" and sum_count[u] == sum_count[n] - 1]
                    if prev:
                        pe.wait_ge(z_by_vector, finish_count[prev[0]])
                    v = product_of(n).rearrange("p (j d) -> p j d", d=D)
                    for o in range(D // OCTANT):
                        last = pe.matmul(fold[:, 0:units[n].pairs * OCTANT].rearrange("p (j d) -> p j d", d=OCTANT),
                                         ident[:, :], v[:, :, o * OCTANT:(o + 1) * OCTANT],
                                         start=(o == 0), stop=(o == D // OCTANT - 1))
                    last.then_inc(folded, 1)

            pe.wait_ge(prod_ready, len(units))
            pe.wait_ge(z_by_vector, len(finish_count))
            if counts["scalar"]:
                pe.wait_ge(z_by_scalar, counts["scalar"])
            pe.wait_ge(dense_loaded, 16)
            pe.wait_ge(mlp_loaded, 6 * 16)
            first = {kind: min(t for t, task in enumerate(mlp) if task[0] == kind) for kind in ("zt", "h1", "h2", "y")}
            evacuated = 0

            def need(t):
                nonlocal evacuated
                if t >= evacuated:
                    for k in range(max(evacuated, t - 1), t + 1):
                        wait_mlp_task(pe, k)
                    evacuated = t + 1

            for t, (kind, n, h) in enumerate(mlp):
                bank = mlp_bank(t)
                half = slice(h * BANK, (h + 1) * BANK)
                if t >= len(mlp_banks):
                    need(t - len(mlp_banks))
                if kind == "zt":
                    rows = min(P, K1 - n * P)
                    for s in range(HALF):
                        last = pe.transpose(bank[0:rows, cols(s)], z[:, h * HALF + s, n * P:n * P + rows], ident[:, :])
                elif kind == "h1":
                    need(first["zt"] + (h + 1) * KT - 1)
                    for k in range(KT):
                        rows = min(P, K1 - k * P)
                        last = pe.matmul(bank, w1_sb[0:rows, k, cols(n)], zt[0:rows, k, half],
                                         start=(k == 0), stop=(k == KT - 1))
                elif kind == "h2":
                    need(first["h1"] + (h + 1) * N1 - 1)
                    for k in range(N1):
                        last = pe.matmul(bank, w2_sb[:, k, cols(n)], h1t[:, k, half],
                                         start=(k == 0), stop=(k == N1 - 1))
                else:
                    need(first["h2"] + (h + 1) * N2 - 1)
                    for k in range(N2):
                        last = pe.matmul(bank[0:1, :], w3_sb[:, k:k + 1], h2t[:, k, half],
                                         start=(k == 0), stop=(k == N2 - 1))
                last.then_inc(mlp_acc, 1)


def kernel(**inputs):
    import numpy as np
    import concourse.bacc as bacc
    from concourse import mybir as mb
    from concourse.bass_utils import run_bass_kernel_spmd as run

    B, F = inputs["ids"].shape
    i_of, j_of = np.triu_indices(F, k=1)
    order = np.lexsort((i_of, j_of))
    W = np.asarray(inputs["L0_rec_W"])
    D = W.shape[1]
    w1 = np.asarray(inputs["W_top1"])
    pairs = len(order)
    arrays = {f"tbl_{f}": np.asarray(inputs[f"tbl_{f}"]) for f in range(F)}
    arrays |= {
        "ids": np.asarray(inputs["ids"]),
        "dense": np.asarray(inputs["dense_ctx"]),
        "weights": W[order].transpose(2, 0, 1).reshape(D, pairs * D),
        "eye": np.eye(P, dtype=np.float32),
        "w1": np.concatenate([w1[order], w1[pairs:]], axis=0),
        "b1": np.asarray(inputs["b_top1"]).reshape(-1, P).T,
        "w2": np.asarray(inputs["W_top2"]),
        "b2": np.asarray(inputs["b_top2"]).reshape(-1, P).T,
        "w3": np.asarray(inputs["W_top3"]).reshape(-1, P).T,
    }
    nc = bacc.Bacc("TRN2", target_bir_lowering=False, num_devices=1)
    arrays = {f"in_{k}": np.ascontiguousarray(a) for k, a in arrays.items()}
    ap = {k: nc.dram_tensor(k, a.shape, mb.dt.from_np(a.dtype), kind="ExternalInput").ap()
          for k, a in arrays.items()}
    out = nc.dram_tensor("out_y", (B, 1), mb.dt.from_np(np.dtype("float32")), kind="ExternalOutput").ap()
    build(nc, [ap[f"in_tbl_{f}"] for f in range(F)], ap["in_ids"], ap["in_dense"], ap["in_weights"], ap["in_eye"],
          ap["in_w1"], ap["in_b1"], ap["in_w2"], ap["in_b2"], ap["in_w3"], out)
    result = run(nc, [arrays], core_ids=[0])
    return result.results[0]["out_y"]
```

```python
from contextlib import ExitStack

import concourse.bass as bass
from concourse import mybir

F32 = mybir.dt.float32
F32R = mybir.dt.float32r
I32 = mybir.dt.int32
ALU = mybir.AluOpType
ACT = mybir.ActivationFunctionType
AX = mybir.AxisListType

P = 128
BANK = 512
PASSES = 2
TURN_BANKS = 2
TURN_SLOTS = 3
PIECE_PAIRS = 20
RAW_SLOTS = 3
PRODUCT_SLOTS = 10
FOLDED = 16
GATHER_AHEAD = 8


class Unit:

    def __init__(self, p, m, tile, tiles, i0, i1):
        self.p, self.m, self.tile, self.tiles, self.i0, self.i1 = p, m, tile, tiles, i0, i1
        self.pairs = tiles * (i1 - i0)
        self.how = "vector"


class Task:

    def __init__(self, kind, p, n, c0, c1):
        self.kind, self.p, self.n, self.c0, self.c1 = kind, p, n, c0, c1


class Plan:

    ENGINES = ("sync", "gpsimd", "scalar", "vector", "tensor")
    SIGNAL = 100.0

    def __init__(self, F, D, B, KT, N1, N2):
        self.F, self.D, self.NB = F, D, B // P // PASSES
        per_bank = BANK // D
        self.units, self.pieces, self.tasks = [], [], []
        self.stages = [(p, m) for p in range(PASSES) for m in range(1, F)]
        self.of_stage = []
        for p, m in self.stages:
            first, t0 = len(self.units), p * self.NB
            if m <= per_bank:
                for t in range(0, self.NB, TURN_BANKS):
                    self.units.append(Unit(p, m, t0 + t, TURN_BANKS, 0, m))
            else:
                parts = -(-m // (TURN_BANKS * per_bank))
                cuts = [m * k // parts for k in range(parts + 1)]
                for t in range(self.NB):
                    self.units += [Unit(p, m, t0 + t, 1, a, b) for a, b in zip(cuts, cuts[1:])]
            self.of_stage.append(range(first, len(self.units)))
        self.stage_of = [s for s, span in enumerate(self.of_stage) for _ in span]
        for m in range(1, F):
            self.pieces += [(m, a, min(a + PIECE_PAIRS, m)) for a in range(0, m, PIECE_PAIRS)]
        for p in range(PASSES):
            width = B // PASSES
            w = width if p == PASSES - 1 else width // 2
            halves = range(0, width, w)
            self.tasks += [Task("zt", p, k, 0, width) for k in range(KT)]
            self.tasks += [Task("h1", p, n, c, c + w) for c in halves for n in range(N1)]
            self.tasks += [Task("h2", p, n, c, c + w) for c in halves for n in range(N2)]
            self.tasks += [Task("y", p, 0, c, c + w) for c in halves]
        self.low_by, self.out_by = {}, {}
        self.turns, self.folds = [], []
        self.order = {e: [] for e in self.ENGINES}
        self.rehearse()

    def pieces_of(self, m):
        return [q for q, piece in enumerate(self.pieces) if piece[0] == m]

    def reader(self, turn):
        kind, n = turn
        return {"unit": ("product", n), "transpose": ("x_low", n), "mlp": ("mlp_out", n)}[kind]

    def rehearse(self):
        F, D, NB = self.F, self.D, self.NB
        units, pieces, stages, tasks = self.units, self.pieces, self.stages, self.tasks
        done = {}
        now = 0.0
        busy = {e: 0.0 for e in self.ENGINES}
        work = {"scalar": 0.0, "tensor": 0.0, "gpsimd": 0.0}
        todo = {k: 0 for k in ("load", "w_high", "x_high", "transpose", "unit", "product", "x_low",
                               "twin", "store", "fetch", "mlp")}
        todo["fetch"] = F - 1
        gathers = [(0, f) for f in range(F)] + [(1, f) for f in range(F)]
        sums = {"scalar": [], "tensor": [], "gpsimd": []}
        finishes, lows, outs = [], [], []
        open_fold = []
        late_loads = ["w1"]

        def have(*steps):
            return all(done.get(step, 1e12) <= now for step in steps)

        def cols(u):
            return units[u].pairs * D

        def units_done(s, kind="unit"):
            return s < 0 or have((kind, self.of_stage[s][-1]))

        def summed(u):
            return u < 0 or have(("sum", u, 0) if units[u].how == "scalar" else ("finish", u))

        def turn_free():
            return len(self.turns) < TURN_SLOTS or have(self.reader(self.turns[-TURN_SLOTS]))

        def lag(u):
            return todo["product"] - u

        def stage_now():
            return self.stage_of[min(todo["product"], len(units) - 1)]

        def sync():
            q = todo["load"]
            if q < len(pieces) and (q < RAW_SLOTS or have(("w_low", q - RAW_SLOTS))):
                return ("load", q), 100, 2200 + 1.5 * (pieces[q][2] - pieces[q][1]) * D
            s = todo["twin"]
            if s < len(stages) and have(("gather", *stages[s])) and (s < 2 or have(("transpose", s - 2))):
                return ("twin", s), 100, 5200
            m = todo["store"] + 1
            if m < F and all(have(("w_low", q)) for q in self.pieces_of(m)):
                return ("store", m), 50, 2500 + 1.6 * m * D
            s = todo["fetch"]
            if s < len(stages) and units_done(s - 2) and have(("store", stages[s][1]), ("store", F - 1)):
                return ("fetch", s), 50, 2500 + 1.6 * stages[s][1] * D
            if late_loads and units_done(F - 2, "product"):
                return ("w1", 0), 100, 8000
            return None

        def gpsimd():
            if gathers:
                p, f = gathers[0]
                if p == 0 or stage_now() >= min(F - 17 + f, F - 1 + f - 14):
                    return ("gather", p, f), NB * 1040, NB * 1040 + 2200
            ready = [u for u in sums["gpsimd"] if have(("product", u))]
            if ready and (lag(ready[0]) > 4 or not lows):
                u = ready[0]
                return ("sum", u, 0), 1.17 * cols(u) + 20, None
            for q in lows:
                if have(("w_high", q)):
                    return ("w_low", q), 2.36 * (pieces[q][2] - pieces[q][1]) * D + 20, None
            if ready:
                return ("sum", ready[0], 0), 1.17 * cols(ready[0]) + 20, None
            if gathers:
                return ("gather", *gathers[0]), NB * 1040, NB * 1040 + 2200
            return None

        def scalar():
            s = todo["x_high"]
            if s < len(stages) and have(("transpose", s)) and units_done(s - 2):
                return ("x_high", s), 0.83 * NB * P + 60, None
            q = todo["w_high"]
            if q < len(pieces) and have(("load", q)):
                m = pieces[q][0]
                if m <= 2 or (units_done(m - 3) and have(("store", m - 2))):
                    return ("w_high", q), 0.83 * (pieces[q][2] - pieces[q][1]) * D + 100, None
            for t in outs:
                if have(("mlp", t)):
                    return ("mlp_out", t), 500, None
            ready = [u for u in sums["scalar"] if have(("product", u))]
            if ready:
                return ("sum", ready[0], 0), 240 * units[ready[0]].pairs, None
            return None

        def vector():
            s = todo["x_low"]
            if s < len(stages) and have(("x_high", s)):
                return ("x_low", s), 610, None
            u = todo["product"]
            s = stage_now()
            for q in lows:
                if have(("w_high", q)) and (pieces[q][0] - 1 <= s or u + 3 >= self.of_stage[s][-1]
                                            or (busy["gpsimd"] > now + 3000 and gathers)):
                    return ("w_low", q), (pieces[q][2] - pieces[q][1]) * D / 0.96 + 70, None
            ready = [f for f in finishes if have(("product", f)) and (
                units[f].how == "vector" or have(("sum", f, 1 if units[f].how == "tensor" else 0)))]
            left = {"vector": 1, "gpsimd": 0.5, "tensor": FOLDED / D}

            def finish(f):
                return ("finish", f), cols(f) * left[units[f].how] / 0.96 + 70, None
            if ready and (lag(ready[0]) > 5 or units[ready[0]].how == "tensor"):
                return finish(ready[0])
            if u < len(units) and have(("unit", u)) and summed(u - PRODUCT_SLOTS) and \
                    have(*[("gather", units[u].p, f) for f in range(units[u].m)]):
                return ("product", u), cols(u) / 0.96 + 70, None
            if ready:
                return finish(ready[0])
            for t in outs:
                if have(("mlp", t)) and busy["scalar"] > now + 600:
                    return ("mlp_out", t), 600, None
            return None

        def tensor():
            s = todo["transpose"]
            if s < len(stages) and have(("twin", s)) and turn_free() and units_done(s - 2) \
                    and stage_now() >= s - 1:
                return ("transpose", s), 440, 700
            u = todo["unit"]
            unit_ok = False
            if u < len(units):
                s = self.stage_of[u]
                p, m = stages[s]
                operands = [("w_low", q) for q in self.pieces_of(m)] if p == 0 else [("fetch", s)]
                unit_ok = turn_free() and have(("x_low", s), *operands)
            folds = open_fold or [f for f in sums["tensor"] if have(("product", f))][:1]
            fold_ok = folds and (open_fold or len(self.folds) < 2 or have(("finish", self.folds[-2])))
            ahead = u - todo["product"]
            if fold_ok and (not unit_ok or ahead >= 2 or lag(folds[0]) > 6):
                half = 1 if open_fold else 0
                return ("sum", folds[0], half), cols(folds[0]) * 0.834 + 20, cols(folds[0]) * 0.834 + 200
            if unit_ok and (ahead < 2 or todo["mlp"] >= len(tasks)):
                return ("unit", u), cols(u) * 0.842, cols(u) * 0.842 + 200
            t = todo["mlp"]
            if t < len(tasks) and turn_free():
                task = tasks[t]
                kinds = ["zt", "h1", "h2", "y"]
                before = [("mlp_out", k) for k in range(t) if tasks[k].p == task.p and k < t
                          and kinds.index(tasks[k].kind) < kinds.index(task.kind)]
                if task.kind == "zt":
                    mine = [v for v in range(len(units)) if units[v].p == task.p]
                    ok = todo["product"] > mine[-1] and all(summed(v) for v in mine) and have(("w1", 0))
                    before += [("mlp_out", k) for k in range(t) if tasks[k].p < task.p]
                else:
                    ok = True
                n = {"zt": 0.85, "h1": 11.8, "h2": 6.8, "y": 3.4}[task.kind] * (task.c1 - task.c0)
                if ok and have(*before):
                    return ("mlp", t), n, n + 200
            if unit_ok:
                return ("unit", u), cols(u) * 0.842, cols(u) * 0.842 + 200
            return None

        def assign(u):
            unit = units[u]
            if unit.tiles > 1 or unit.m <= 8:
                return "vector"
            spare = {"scalar": busy["scalar"] - now + work["scalar"],
                     "tensor": 2.6 * work["tensor"],
                     "gpsimd": max(busy["gpsimd"] - now, 0) + work["gpsimd"]}
            cost = {"scalar": 240 * unit.pairs, "tensor": 1.67 * cols(u), "gpsimd": 1.17 * cols(u)}
            if gathers and (gathers[0][0] == 0):
                spare["gpsimd"] = 1e9
            late = {e: (max(spare[e], 0) + cost[e]) / SUM_HORIZON[e] for e in spare}
            best = min(late, key=late.get)
            return best if late[best] < 1 else "vector"

        pick = {"sync": sync, "gpsimd": gpsimd, "scalar": scalar, "vector": vector, "tensor": tensor}
        events = []
        while True:
            for e in self.ENGINES:
                if busy[e] > now:
                    continue
                found = pick[e]()
                if found is None:
                    continue
                step, cost, latency = found
                busy[e] = now + cost
                ready = now + (latency or cost) + self.SIGNAL
                done[step] = ready
                events += [busy[e], ready]
                self.order[e].append(step)
                kind, n = step[:2]
                if kind in todo:
                    todo[kind] += 1
                if kind in ("unit", "transpose", "mlp"):
                    self.turns.append((kind, n))
                if kind == "w_high":
                    lows.append(n)
                elif kind == "w_low":
                    lows.remove(n)
                    self.low_by[n] = e
                elif kind == "mlp":
                    outs.append(n)
                elif kind == "mlp_out":
                    outs.remove(n)
                    self.out_by[n] = e
                elif kind == "gather":
                    gathers.remove((n, step[2]))
                elif kind == "w1":
                    late_loads.clear()
                elif kind == "product":
                    how = units[n].how = assign(n)
                    if how != "scalar":
                        finishes.append(n)
                    if how != "vector":
                        sums[how].append(n)
                        work[how] += {"scalar": 240 * units[n].pairs, "tensor": 1.67 * cols(n),
                                      "gpsimd": 1.17 * cols(n)}[how]
                elif kind == "finish":
                    finishes.remove(n)
                elif kind == "sum":
                    how = units[n].how
                    work[how] -= cost
                    if how == "tensor" and step[2] == 0:
                        open_fold.append(n)
                        self.folds.append(n)
                    else:
                        open_fold.clear() if how == "tensor" else None
                        sums[how].remove(n)
            events = sorted({t for t in events if t > now})
            if not events:
                break
            now = events[0]
        self.end = now
        self.done = done
        assert todo["mlp"] == len(tasks) and not outs, "the rehearsal got stuck"


SUM_HORIZON = {"scalar": 12000, "tensor": 3000, "gpsimd": 3000}


def build(nc, tables, ids, dense, weights, eye, w1, b1, w2, b2, w3, scratch, out):
    B, F = ids.shape
    D = tables[0].shape[1]
    TILES = B // P
    NB = TILES // PASSES
    WIDTH = NB * P
    PAIRS = F * (F - 1) // 2
    H1, H2 = w2.shape
    K1 = w1.shape[0]
    KT = -(-K1 // P)
    N1, N2 = H1 // P, H2 // P
    assert WIDTH == BANK
    plan = Plan(F, D, B, KT, N1, N2)
    units, pieces, of_stage, stages, tasks = plan.units, plan.pieces, plan.of_stage, plan.stages, plan.tasks
    base = [m * (m - 1) // 2 for m in range(F + 1)]

    with ExitStack() as ctx:
        def sb(name, shape, dt=F32):
            return ctx.enter_context(nc.sbuf_tensor(name, shape, dt))

        def ps(name, shape):
            return ctx.enter_context(nc.psum_tensor(name, shape, F32))

        def sem(name):
            return ctx.enter_context(nc.semaphore(name))

        idx = sb("idx", [P, TILES, F], I32)
        emb = sb("emb", [P, TILES, F * D])
        ident = sb("ident", [P, P])
        raw = sb("raw", [P, RAW_SLOTS, PIECE_PAIRS * D])
        wsplit = sb("wsplit", [P, 2, (F - 1) * D], F32R)
        twin = sb("twin", [P, 2, NB, 2, D])
        xsplit = sb("xsplit", [P, 2, 2, WIDTH], F32R)
        prod = sb("prod", [P, PRODUCT_SLOTS, TURN_BANKS * BANK])
        z = sb("z", [P, TILES, K1])
        w2_sb = sb("w2_sb", [P, N1, H2])
        w3_sb = sb("w3_sb", [P, N2])
        b1_sb = sb("b1_sb", [P, N1])
        b2_sb = sb("b2_sb", [P, N2])
        y_sb = sb("y_sb", [1, B])
        free = emb[:, 0:NB, :].rearrange("p t c -> p (t c)")
        at = [0, KT * H1, KT * (H1 + WIDTH), KT * (H1 + WIDTH) + N1 * WIDTH,
              KT * (H1 + WIDTH) + (N1 + N2) * WIDTH]
        assert at[-1] <= NB * F * D
        w1_sb = free[:, at[0]:at[1]].rearrange("p (k n) -> p k n", k=KT)
        zt = free[:, at[1]:at[2]].rearrange("p (k b) -> p k b", k=KT)
        h1t = free[:, at[2]:at[3]].rearrange("p (k b) -> p k b", k=N1)
        h2t = free[:, at[3]:at[4]].rearrange("p (k b) -> p k b", k=N2)

        uacc = ps("uacc", [P, TURN_SLOTS, TURN_BANKS, BANK])
        fold = ps("fold", [P, 2, BANK])

        idx_loaded = sem("idx_loaded")
        ident_loaded = sem("ident_loaded")
        mlp_loaded = sem("mlp_loaded")
        gathered = [[sem(f"gathered{p}_{m}") for m in range(F)] for p in range(PASSES)]
        raw_loaded = [sem(f"raw_loaded{s}") for s in range(RAW_SLOTS)]
        twin_copied = [sem(f"twin_copied{s}") for s in range(2)]
        w_stored = [sem(f"w_stored{s}") for s in range(2)]
        w_fetched = [sem(f"w_fetched{s}") for s in range(2)]
        w_high_done = sem("w_high_done")
        w_low_by = {"vector": sem("w_low_by_vector"), "gpsimd": sem("w_low_by_gpsimd")}
        x_transposed = sem("x_transposed")
        x_high_done = sem("x_high_done")
        x_low_done = sem("x_low_done")
        u_ready = sem("u_ready")
        prod_ready = sem("prod_ready")
        halved = sem("halved")
        folded = sem("folded")
        z_by_vector = sem("z_by_vector")
        z_by_scalar = sem("z_by_scalar")
        mlp_acc = sem("mlp_acc")
        mlp_out_by = {"scalar": sem("mlp_out_by_scalar"), "vector": sem("mlp_out_by_vector")}
        out_stored = sem("out_stored")

        def count(steps):
            return {step[1]: k + 1 for k, step in enumerate(steps)}

        order = plan.order
        finish_count = count([step for step in order["vector"] if step[0] == "finish"])
        sum_count, low_count, out_count = {}, {}, {}
        for e in ("gpsimd", "scalar", "vector", "tensor"):
            sum_count |= count([step for step in order[e] if step[0] == "sum" and step[2] == (e == "tensor")])
            low_count |= count([step for step in order[e] if step[0] == "w_low"])
            out_count |= count([step for step in order[e] if step[0] == "mlp_out"])
        turns = plan.turns
        turn_of = {turn: t for t, turn in enumerate(turns)}
        folds = plan.folds

        def wait_low(eng, q):
            eng.wait_ge(w_low_by[plan.low_by[q]], low_count[q])

        def wait_lows(eng, m):
            for q in plan.pieces_of(m):
                wait_low(eng, q)

        def wait_task(eng, t):
            eng.wait_ge(mlp_out_by[plan.out_by[t]], out_count[t])

        def wait_summed(eng, u):
            if units[u].how == "scalar":
                eng.wait_ge(z_by_scalar, sum_count[u])
            else:
                eng.wait_ge(z_by_vector, finish_count[u])

        def wait_z(eng, p):
            mine = [u for u in range(len(units)) if units[u].p == p]
            eng.wait_ge(z_by_vector, max(finish_count[u] for u in mine if u in finish_count))
            eng.wait_ge(z_by_scalar, max(sum_count[u] for u in mine if units[u].how == "scalar"))

        def z_of(unit):
            c = base[unit.m] + unit.i0
            return z[:, unit.tile:unit.tile + unit.tiles, c:c + unit.i1 - unit.i0]

        def product_of(u):
            return prod[:, u % PRODUCT_SLOTS, 0:units[u].pairs * D]

        def acc(kind, n):
            return uacc[:, turn_of[kind, n] % TURN_SLOTS, :, :]

        def split_low(eng, q):
            m, a, b = pieces[q]
            eng.wait_ge(w_high_done, q + 1)
            w = wsplit[0:D, (m - 1) % 2, a * D:b * D]
            eng.tensor_tensor(w, raw[0:D, q % RAW_SLOTS, 0:(b - a) * D], w.bitcast(F32),
                              ALU.subtract).then_inc(w_low_by[plan.low_by[q]], 1)

        block = ctx.enter_context(nc.Block())

        @block.sync
        def _(sp):
            sp.dma_start(idx[:, :, :], ids.rearrange("(t p) f -> p t f", p=P)).then_inc(idx_loaded, 16)
            sp.dma_start(ident[:, :], eye).then_inc(ident_loaded, 16)
            for kind, n, *_ in order["sync"]:
                if kind == "load":
                    m, a, b = pieces[n]
                    if n >= RAW_SLOTS:
                        wait_low(sp, n - RAW_SLOTS)
                    for half in range(2):
                        sp.dma_start(raw[half * D:(half + 1) * D, n % RAW_SLOTS, 0:(b - a) * D],
                                     weights[:, (base[m] + a) * D:(base[m] + b) * D]
                                     ).then_inc(raw_loaded[n % RAW_SLOTS], 16)
                elif kind == "twin":
                    p, m = stages[n]
                    sp.wait_ge(gathered[p][m], 16 * NB)
                    if n >= 2:
                        sp.wait_ge(x_transposed, n - 1)
                    if n == 1:
                        sp.dma_start(z[:, :, PAIRS:K1], dense.rearrange("(t p) f -> p t f", p=P)
                                     ).then_inc(mlp_loaded, 16)
                        sp.dma_start(w2_sb[:, :, :], w2.rearrange("(k p) n -> p k n", p=P)).then_inc(mlp_loaded, 16)
                        sp.dma_start(w3_sb[:, :], w3).then_inc(mlp_loaded, 16)
                        sp.dma_start(b1_sb[:, :], b1).then_inc(mlp_loaded, 16)
                        sp.dma_start(b2_sb[:, :], b2).then_inc(mlp_loaded, 16)
                    for k in range(2):
                        sp.dma_start(twin[:, n % 2, :, k, :], emb[:, p * NB:(p + 1) * NB, m * D:(m + 1) * D]
                                     ).then_inc(twin_copied[n % 2], 16)
                elif kind == "store":
                    wait_lows(sp, n)
                    sp.dma_start(scratch[:, base[n] * D:base[n + 1] * D], wsplit[:, (n - 1) % 2, 0:n * D].bitcast(F32)
                                 ).then_inc(w_stored[(n - 1) % 2], 16)
                elif kind == "fetch":
                    p, m = stages[n]
                    sp.wait_ge(w_stored[(m - 1) % 2], 16 * ((m - 1) // 2 + 1))
                    if m <= 2:
                        for slot in range(2):
                            sp.wait_ge(w_stored[slot], 16 * len([k for k in range(1, F) if (k - 1) % 2 == slot]))
                    sp.wait_ge(u_ready, of_stage[n - 2][-1] + 1)
                    sp.dma_start(wsplit[:, n % 2, 0:m * D].bitcast(F32), scratch[:, base[m] * D:base[m + 1] * D]
                                 ).then_inc(w_fetched[n % 2], 16)
                elif kind == "w1":
                    sp.wait_ge(prod_ready, of_stage[F - 2][-1] + 1)
                    full = K1 // P
                    sp.dma_start(w1_sb[:, 0:full, :], w1[0:full * P, :].rearrange("(k p) n -> p k n", p=P)
                                 ).then_inc(mlp_loaded, 16)
                    sp.dma_start(w1_sb[0:K1 - full * P, full, :], w1[full * P:K1, :]).then_inc(mlp_loaded, 16)
            for t, task in enumerate(tasks):
                if task.kind == "y":
                    wait_task(sp, t)
            sp.dma_start(out.rearrange("b o -> o b"), y_sb[:, :]).then_inc(out_stored, 16)
            sp.wait_ge(out_stored, 16)

        @block.gpsimd
        def _(pool):
            pool.wait_ge(idx_loaded, 16)
            for kind, n, *rest in order["gpsimd"]:
                if kind == "gather":
                    m = rest[0]
                    for t in range(n * NB, (n + 1) * NB):
                        pool.indirect_dma_start(
                            emb[:, t, m * D:(m + 1) * D], None, tables[m][:, :],
                            bass.IndirectOffsetOnAxis(ap=idx[:, t, m:m + 1], axis=0)).then_inc(gathered[n][m], 16)
                elif kind == "w_low":
                    split_low(pool, n)
                elif kind == "sum":
                    v = product_of(n).rearrange("p (j d) -> p j d", d=D)
                    pool.wait_ge(prod_ready, n + 1)
                    pool.tensor_tensor(v[:, :, 0:D // 2], v[:, :, 0:D // 2], v[:, :, D // 2:D],
                                       ALU.add).then_inc(halved, 1)

        @block.scalar
        def _(act):
            for kind, n, *rest in order["scalar"]:
                if kind == "w_high":
                    m, a, b = pieces[n]
                    act.wait_ge(raw_loaded[n % RAW_SLOTS], 32 * (n // RAW_SLOTS + 1))
                    if m > 2:
                        act.wait_ge(u_ready, of_stage[m - 3][-1] + 1)
                        act.wait_ge(w_stored[(m - 1) % 2], 16 * ((m - 1) // 2))
                    act.activation(wsplit[:, (m - 1) % 2, a * D:b * D], raw[:, n % RAW_SLOTS, 0:(b - a) * D],
                                   ACT.Copy).then_inc(w_high_done, 1)
                elif kind == "x_high":
                    act.wait_ge(x_transposed, n + 1)
                    if n >= 2:
                        act.wait_ge(u_ready, of_stage[n - 2][-1] + 1)
                    act.activation(xsplit[:, n % 2, 0, :], acc("transpose", n)[:, 0, :],
                                   ACT.Copy).then_inc(x_high_done, 1)
                elif kind == "sum":
                    unit = units[n]
                    act.wait_ge(prod_ready, n + 1)
                    zv, pv = z_of(unit), product_of(n)
                    for j in range(unit.pairs):
                        last = act.activation(pv[:, j * D:(j + 1) * D], pv[:, j * D:(j + 1) * D], ACT.Copy,
                                              accum_out=zv[:, 0, j:j + 1])
                    last.then_inc(z_by_scalar, 1)
                elif kind == "mlp_out":
                    task = tasks[n]
                    act.wait_ge(mlp_acc, n + 1)
                    act.wait_ge(mlp_loaded, 7 * 16)
                    cols = slice(task.c0, task.c1)
                    rows = min(P, K1 - task.n * P)
                    src = acc("mlp", n)[:, 0, 0:task.c1 - task.c0]
                    if task.kind == "zt":
                        ins = act.activation(zt[0:rows, task.n, cols], src[0:rows, :], ACT.Copy)
                    elif task.kind == "h1":
                        ins = act.activation(h1t[:, task.n, cols], src, ACT.Relu, bias=b1_sb[:, task.n:task.n + 1])
                    elif task.kind == "h2":
                        ins = act.activation(h2t[:, task.n, cols], src, ACT.Relu, bias=b2_sb[:, task.n:task.n + 1])
                    else:
                        y = y_sb[0:1, task.p * WIDTH + task.c0:task.p * WIDTH + task.c1]
                        ins = act.activation(y, src[0:1, :], ACT.Copy)
                    ins.then_inc(mlp_out_by["scalar"], 1)

        @block.vector
        def _(dve):
            seen = [0] * PASSES
            for kind, n, *rest in order["vector"]:
                if kind == "w_low":
                    split_low(dve, n)
                elif kind == "x_low":
                    dve.wait_ge(x_high_done, n + 1)
                    dve.tensor_tensor(xsplit[:, n % 2, 1, :], acc("transpose", n)[:, 0, :],
                                      xsplit[:, n % 2, 0, :].bitcast(F32), ALU.subtract).then_inc(x_low_done, 1)
                elif kind == "product":
                    unit = units[n]
                    while seen[unit.p] < unit.m:
                        dve.wait_ge(gathered[unit.p][seen[unit.p]], 16 * NB)
                        seen[unit.p] += 1
                    dve.wait_ge(u_ready, n + 1)
                    if n >= PRODUCT_SLOTS:
                        wait_summed(dve, n - PRODUCT_SLOTS)
                    width = (unit.i1 - unit.i0) * D
                    e = emb[:, unit.tile:unit.tile + unit.tiles, unit.i0 * D:unit.i1 * D]
                    if unit.tiles == 1:
                        u_in = acc("unit", n).rearrange("p c n -> p (c n)")[:, 0:width]
                        dve.tensor_tensor(product_of(n), u_in, e[:, 0, :], ALU.mult).then_inc(prod_ready, 1)
                    else:
                        dve.tensor_tensor(product_of(n).rearrange("p (t c) -> p t c", t=unit.tiles),
                                          acc("unit", n)[:, 0:unit.tiles, 0:width], e,
                                          ALU.mult).then_inc(prod_ready, 1)
                elif kind == "finish":
                    unit = units[n]
                    if unit.how == "tensor":
                        dve.wait_ge(folded, sum_count[n])
                        v = fold[:, (sum_count[n] - 1) % 2, 0:unit.pairs * FOLDED].rearrange(
                            "p (t j d) -> p t j d", t=unit.tiles, d=FOLDED)
                    else:
                        v = product_of(n).rearrange("p (t j d) -> p t j d", t=unit.tiles, d=D)
                        if unit.how == "gpsimd":
                            dve.wait_ge(halved, sum_count[n])
                            v = v[:, :, :, 0:D // 2]
                        else:
                            dve.wait_ge(prod_ready, n + 1)
                    dve.tensor_reduce(z_of(unit), v, AX.X, ALU.add).then_inc(z_by_vector, 1)
                elif kind == "mlp_out":
                    task = tasks[n]
                    dve.wait_ge(mlp_acc, n + 1)
                    dve.wait_ge(mlp_loaded, 7 * 16)
                    cols = slice(task.c0, task.c1)
                    rows = min(P, K1 - task.n * P)
                    src = acc("mlp", n)[:, 0, 0:task.c1 - task.c0]
                    if task.kind == "zt":
                        ins = dve.tensor_copy(zt[0:rows, task.n, cols], src[0:rows, :])
                    elif task.kind == "h1":
                        ins = dve.tensor_scalar(h1t[:, task.n, cols], src, b1_sb[:, task.n:task.n + 1], 0.0,
                                                ALU.add, ALU.max)
                    elif task.kind == "h2":
                        ins = dve.tensor_scalar(h2t[:, task.n, cols], src, b2_sb[:, task.n:task.n + 1], 0.0,
                                                ALU.add, ALU.max)
                    else:
                        y = y_sb[0:1, task.p * WIDTH + task.c0:task.p * WIDTH + task.c1]
                        ins = dve.tensor_copy(y, src[0:1, :])
                    ins.then_inc(mlp_out_by["vector"], 1)

        @block.tensor
        def _(pe):
            pe.wait_ge(ident_loaded, 16)

            def take_turn(kind, n):
                t = turn_of[kind, n] - TURN_SLOTS
                if t >= 0:
                    kind, n = turns[t]
                    if kind == "unit":
                        pe.wait_ge(prod_ready, n + 1)
                    elif kind == "transpose":
                        pe.wait_ge(x_low_done, n + 1)
                    else:
                        wait_task(pe, n)

            def wait_operand(p, kind, col, t):
                for k, task in enumerate(tasks[:t]):
                    if task.p == p and task.kind == kind and task.c0 <= col < task.c1:
                        wait_task(pe, k)

            for kind, n, *rest in order["tensor"]:
                if kind == "transpose":
                    pe.wait_ge(twin_copied[n % 2], 32 * (n // 2 + 1))
                    take_turn(kind, n)
                    for t in range(NB):
                        last = pe.transpose(acc(kind, n)[:, 0, t * P:(t + 1) * P],
                                            twin[:, n % 2, t, :, :].rearrange("p k d -> p (k d)"), ident[:, :])
                    last.then_inc(x_transposed, 1)
                elif kind == "unit":
                    unit = units[n]
                    s = unit.p * (F - 1) + unit.m - 1
                    if n == of_stage[s][0]:
                        pe.wait_ge(x_low_done, s + 1)
                        if unit.p == 0:
                            wait_lows(pe, unit.m)
                        else:
                            before = (F - 1 + 1 - s % 2) // 2
                            pe.wait_ge(w_fetched[s % 2], 16 * (s // 2 + 1 - before))
                    take_turn(kind, n)
                    width = (unit.i1 - unit.i0) * D
                    for t in range(unit.tiles):
                        b0 = (unit.tile + t) % NB * P
                        for part in range(2):
                            for c in range(0, width, BANK):
                                w = min(BANK, width - c)
                                last = pe.matmul(acc(kind, n)[:, t + c // BANK, 0:w],
                                                 xsplit[:, s % 2, part, b0:b0 + P],
                                                 wsplit[:, s % 2, unit.i0 * D + c:unit.i0 * D + c + w],
                                                 start=(part == 0), stop=(part == 1))
                    last.then_inc(u_ready, 1)
                elif kind == "sum":
                    half = rest[0]
                    k = folds.index(n)
                    if half == 0:
                        pe.wait_ge(prod_ready, n + 1)
                        if k >= 2:
                            pe.wait_ge(z_by_vector, finish_count[folds[k - 2]])
                    v = product_of(n).rearrange("p (j d) -> p j d", d=D)
                    dst = fold[:, k % 2, 0:units[n].pairs * FOLDED].rearrange("p (j d) -> p j d", d=FOLDED)
                    parts = D // FOLDED
                    for o in range(half * parts // 2, (half + 1) * parts // 2):
                        last = pe.matmul(dst, ident[:, :], v[:, :, o * FOLDED:(o + 1) * FOLDED],
                                         start=(o == 0), stop=(o == parts - 1))
                    if half == 1:
                        last.then_inc(folded, 1)
                elif kind == "mlp":
                    task = tasks[n]
                    if task.kind == "zt" and task.n == 0:
                        wait_z(pe, task.p)
                        pe.wait_ge(mlp_loaded, 7 * 16)
                        if task.p:
                            for k in range(n - 2, n):
                                wait_task(pe, k)
                    take_turn(kind, n)
                    dst = acc(kind, n)[:, 0, 0:task.c1 - task.c0]
                    cols = slice(task.c0, task.c1)
                    if task.kind == "zt":
                        rows = min(P, K1 - task.n * P)
                        for t in range(NB):
                            last = pe.transpose(dst[0:rows, t * P:(t + 1) * P],
                                                z[:, task.p * NB + t, task.n * P:task.n * P + rows], ident[:, :])
                    elif task.kind == "h1":
                        wait_operand(task.p, "zt", task.c0, n)
                        for k in range(KT):
                            rows = min(P, K1 - k * P)
                            last = pe.matmul(dst, w1_sb[0:rows, k, task.n * P:(task.n + 1) * P], zt[0:rows, k, cols],
                                             start=(k == 0), stop=(k == KT - 1))
                    elif task.kind == "h2":
                        wait_operand(task.p, "h1", task.c0, n)
                        for k in range(N1):
                            last = pe.matmul(dst, w2_sb[:, k, task.n * P:(task.n + 1) * P], h1t[:, k, cols],
                                             start=(k == 0), stop=(k == N1 - 1))
                    else:
                        wait_operand(task.p, "h2", task.c0, n)
                        for k in range(N2):
                            last = pe.matmul(dst[0:1, :], w3_sb[:, k:k + 1], h2t[:, k, cols],
                                             start=(k == 0), stop=(k == N2 - 1))
                    last.then_inc(mlp_acc, 1)


def kernel(**inputs):
    import numpy as np
    import concourse.bacc as bacc
    from concourse import mybir as mb
    from concourse.bass_utils import run_bass_kernel_spmd as run

    B, F = inputs["ids"].shape
    i_of, j_of = np.triu_indices(F, k=1)
    order = np.lexsort((i_of, j_of))
    W = np.asarray(inputs["L0_rec_W"])
    D = W.shape[1]
    w1 = np.asarray(inputs["W_top1"])
    pairs = len(order)
    arrays = {f"tbl_{f}": np.asarray(inputs[f"tbl_{f}"]) for f in range(F)}
    arrays |= {
        "ids": np.asarray(inputs["ids"]),
        "dense": np.asarray(inputs["dense_ctx"]),
        "weights": W[order].transpose(2, 0, 1).reshape(D, pairs * D),
        "eye": np.eye(P, dtype=np.float32),
        "w1": np.concatenate([w1[order], w1[pairs:]], axis=0),
        "b1": np.asarray(inputs["b_top1"]).reshape(-1, P).T,
        "w2": np.asarray(inputs["W_top2"]),
        "b2": np.asarray(inputs["b_top2"]).reshape(-1, P).T,
        "w3": np.asarray(inputs["W_top3"]).reshape(-1, P).T,
    }
    nc = bacc.Bacc("TRN2", target_bir_lowering=False, num_devices=1)
    arrays = {f"in_{k}": np.ascontiguousarray(a) for k, a in arrays.items()}
    ap = {k: nc.dram_tensor(k, a.shape, mb.dt.from_np(a.dtype), kind="ExternalInput").ap()
          for k, a in arrays.items()}
    out = nc.dram_tensor("out_y", (B, 1), mb.dt.from_np(np.dtype("float32")), kind="ExternalOutput").ap()
    scratch = nc.dram_tensor("split_weights", (P, pairs * D), mb.dt.float32, kind="Internal").ap()
    build(nc, [ap[f"in_tbl_{f}"] for f in range(F)], ap["in_ids"], ap["in_dense"], ap["in_weights"], ap["in_eye"],
          ap["in_w1"], ap["in_b1"], ap["in_w2"], ap["in_b2"], ap["in_w3"], scratch, out)
    result = run(nc, [arrays], core_ids=[0])
    return result.results[0]["out_y"]
```

```python
from contextlib import ExitStack

import concourse.bass as bass
from concourse import mybir

F32 = mybir.dt.float32
F32R = mybir.dt.float32r
I32 = mybir.dt.int32
ALU = mybir.AluOpType
ACT = mybir.ActivationFunctionType
AX = mybir.AxisListType

P = 128
BANK = 512
HALVES = 2
PASSES = ((0, 4), (4, 8))
TURN_BANKS = 2
TURN_SLOTS = 3
PIECE_PAIRS = 20
RAW_SLOTS = 3
PRODUCT_SLOTS = 10
FOLDED = 16
SCALAR_PAIRS = 4
X_SLOTS = 3
W_SEMAPHORES = 12
VECTOR_SPLITS = 8

SLOW_STAGES = (9, 3)
GATHER_AHEAD = 4
UNITS_AHEAD = 2
LAG = {"gpsimd": 2, "vector": 8, "tensor": 8}
LOW_UNITS = 1
EAGER_PIECES = 20
DIRECT_SUMS = (4, 9)
MLP_FROM, MLP_PACE = 11, 0.8
SUM_HORIZON = ({"scalar": 8000, "tensor": 2000, "gpsimd": 3000},
               {"scalar": 14000, "tensor": 2000, "gpsimd": 6000})
TWO_HALVINGS = 2000


class Unit:

    def __init__(self, p, m, tile, tiles, i0, i1):
        self.p, self.m, self.tile, self.tiles, self.i0, self.i1 = p, m, tile, tiles, i0, i1
        self.pairs = tiles * (i1 - i0)
        self.how = "vector"
        self.halvings = 1


class Task:

    def __init__(self, kind, p, n, c0, c1, k0=0, k1=None):
        self.kind, self.p, self.n, self.c0, self.c1 = kind, p, n, c0, c1
        self.k0, self.k1 = k0, k1


class Plan:

    ENGINES = ("sync", "gpsimd", "scalar", "vector", "tensor")
    SIGNAL = 100.0

    def __init__(self, F, D, B, KT, N1, N2):
        self.F, self.D, self.NB = F, D, B // P // HALVES
        assert PASSES[-1][1] == B // P
        per_bank = BANK // D
        self.units, self.pieces, self.tasks = [], [], []
        self.first_half = sum(t1 <= self.NB for _, t1 in PASSES)
        self.stages = [(p, m) for p in range(len(PASSES)) for m in range(1, F)]
        self.of_stage = []
        for p, m in self.stages:
            first = len(self.units)
            if m <= per_bank + 1:
                cuts = [0, m] if m <= per_bank else [0, m // 2, m]
                for t in range(*PASSES[p], TURN_BANKS):
                    self.units += [Unit(p, m, t, TURN_BANKS, a, b) for a, b in zip(cuts, cuts[1:])]
            else:
                parts = -(-m // (TURN_BANKS * per_bank))
                cuts = [m * k // parts for k in range(parts + 1)]
                if cuts[1] in (per_bank, per_bank + 1):
                    cuts[1] = m - per_bank - 2
                for t in range(*PASSES[p]):
                    self.units += [Unit(p, m, t, 1, a, b) for a, b in zip(cuts, cuts[1:])]
            self.of_stage.append(range(first, len(self.units)))
        self.stage_of = [s for s, span in enumerate(self.of_stage) for _ in span]
        for m in range(1, F):
            self.pieces += [(m, a, min(a + PIECE_PAIRS, m)) for a in range(0, m, PIECE_PAIRS)]
        for p in range(HALVES):
            width = B // HALVES
            w, cut = width // 2, 0
            if p < HALVES - 1:
                self.tasks += [Task("zt", p, k, 0, width) for k in range(KT)]
            else:
                cut = (F - 2) * (F - 3) // 2 // P
                self.late_tasks = len(self.tasks) + cut + N1
                self.tasks += [Task("zt", p, k, 0, width) for k in range(cut)]
                self.tasks += [Task("h1_part", p, n, 0, width, 0, cut) for n in range(N1)]
            for c in range(0, width, w):
                if cut:
                    self.tasks += [Task("zt", p, k, c, c + w) for k in range(cut, KT)]
                self.tasks += [Task("h1", p, n, c, c + w, cut, KT) for n in range(N1)]
                self.tasks += [Task("h2", p, n, c, c + w) for n in range(N2)]
                self.tasks += [Task("y", p, 0, c, c + w)]
        half, self.place = F - 1, {}
        low, at = half, half
        for m in range(1, F):
            if at + m > low + half or m > half // 2:
                low = half - low
                at = low
            self.place[m] = at
            at += m
        self.low_by, self.out_by = {}, {}
        self.turns, self.folds = [], []
        self.order = {e: [] for e in self.ENGINES}
        self.rehearse()

    def x_on_vector(self, s):
        return s < VECTOR_SPLITS

    def w_at(self, m):
        return self.place[m]

    def overwritten(self, s):
        m = self.stages[s][1]
        mine, found = set(range(self.w_at(m), self.w_at(m) + m)), []
        for k in range(s - 1, -1, -1):
            n = self.stages[k][1]
            theirs = mine & set(range(self.w_at(n), self.w_at(n) + n))
            if theirs:
                found.append(k)
                mine -= theirs
            if not mine:
                break
        return found

    def pieces_of(self, m):
        return [q for q, piece in enumerate(self.pieces) if piece[0] == m]

    def zt_needs(self, task):
        first = task.p * self.NB
        return [u for u, unit in enumerate(self.units)
                if task.c0 // P <= unit.tile - first < -(-task.c1 // P) and unit.m * (unit.m - 1) // 2 < (task.n + 1) * P]

    def tiles_of(self, p):
        return PASSES[p][1] - PASSES[p][0]

    def reader(self, turn):
        kind, n = turn
        return {"unit": ("product", n), "transpose": ("x_low", n), "mlp": ("mlp_out", n)}[kind]

    def rehearse(self):
        F, D, NB = self.F, self.D, self.NB
        units, pieces, stages, tasks = self.units, self.pieces, self.stages, self.tasks
        done = {}
        now = 0.0
        busy = {e: 0.0 for e in self.ENGINES}
        busy["gpsimd"] = 3500.0
        work = {"scalar": 0.0, "tensor": 0.0, "gpsimd": 0.0}
        todo = {k: 0 for k in ("load", "w_high", "x_high", "transpose", "unit", "product", "x_low",
                               "x_cut", "twin", "store", "fetch", "mlp")}
        todo["fetch"] = F - 1
        gathers = [(p, f, t) for p in range(len(PASSES)) for f in (1, 0, *range(2, F)) for t in range(*PASSES[p])]
        sums = {"scalar": [], "tensor": [], "gpsimd": []}
        finishes, lows, outs = [], [], []
        open_fold = []
        dma_free = [3000.0]
        late_loads = ["w1"]
        summing = []

        def have(*steps):
            return all(done.get(step, 1e12) <= now for step in steps)

        def cols(u):
            return units[u].pairs * D

        def units_done(s, kind="unit"):
            return s < 0 or have((kind, self.of_stage[s][-1]))

        def summed(u):
            return u < 0 or have(("sum", u, 0) if units[u].how == "scalar" else ("finish", u))

        def turn_free():
            return len(self.turns) < TURN_SLOTS or have(self.reader(self.turns[-TURN_SLOTS]))

        def lag(u):
            return todo["product"] - u

        def stage_now():
            return self.stage_of[min(todo["product"], len(units) - 1)]

        def dma(issue, *durations):
            for k, duration in enumerate(durations):
                dma_free[0] = max(dma_free[0], now + (k + 1) * issue + 650) + duration
            return issue * len(durations), dma_free[0] + 930 - now

        def sync():
            s = todo["twin"]
            if s < len(stages) and have(("gather", *stages[s])) and (s < X_SLOTS or have(("transpose", s - X_SLOTS))):
                return ("twin", s), *dma(650, *[182 * self.tiles_of(stages[s][0])] * 2)
            q = todo["load"]
            if q < len(pieces) and (q < RAW_SLOTS or have(("w_low", q - RAW_SLOTS))):
                return ("load", q), *dma(475, max(360, 1.42 * (pieces[q][2] - pieces[q][1]) * D))
            m = todo["store"] + 1
            if m < F and all(have(("w_low", q)) for q in self.pieces_of(m)):
                return ("store", m), *dma(475, 1.42 * m * D)
            s = todo["fetch"]
            if s < len(stages) and units_done(max(self.overwritten(s))) and have(("store", stages[s][1])) \
                    and have(*[("store", k + 1) for k in self.overwritten(s) if k < F - 1]):
                return ("fetch", s), *dma(475, 1.42 * stages[s][1] * D)
            if late_loads and units_done(self.first_half * (F - 1) + 9, "product"):
                return ("w1", 0), 4000, 8000
            return None

        def halving(u):
            return (2.34 - 2.34 / 2 ** units[u].halvings) * cols(u) + 30 * units[u].halvings

        def gpsimd():
            if gathers:
                p, f, _ = gathers[0]
                if p == 0 or stage_now() >= p * (F - 1) + f - GATHER_AHEAD:
                    return ("gather", *gathers[0]), 1040, 2800
            ready = [u for u in sums["gpsimd"] if have(("product", u))]
            if ready and (lag(ready[0]) > LAG["gpsimd"] or not lows):
                u = ready[0]
                return ("sum", u, 0), halving(u), None
            for q in lows:
                if have(("w_high", q)):
                    return ("w_low", q), 2.36 * (pieces[q][2] - pieces[q][1]) * D + 20, None
            if ready:
                return ("sum", ready[0], 0), halving(ready[0]), None
            if gathers:
                return ("gather", *gathers[0]), 1040, 2800
            return None

        def scalar():
            s = todo["x_high"]
            if s < len(stages) and have(("transpose", s)) and units_done(s - X_SLOTS):
                return ("x_high", s), 0.83 * self.tiles_of(stages[s][0]) * P + 60, None
            s = todo["x_low"]
            if s < len(stages) and not self.x_on_vector(s) and have(("x_cut", s)):
                return ("x_low", s), 0.83 * self.tiles_of(stages[s][0]) * P + 60, None
            q = todo["w_high"]
            if q < len(pieces) and have(("load", q)):
                m = pieces[q][0]
                if all(units_done(k) and have(("store", k + 1)) for k in self.overwritten(m - 1)):
                    return ("w_high", q), 0.83 * (pieces[q][2] - pieces[q][1]) * D + 100, None
            for t in outs:
                if have(("mlp", t)):
                    return ("mlp_out", t), 500, None
            ready = [u for u in sums["scalar"] if have(("product", u))]
            if ready and not summing:
                summing.append(units[ready[0]].pairs)
            if ready:
                n = min(SCALAR_PAIRS, summing[0])
                return ("sum", ready[0], summing[0] - n), 240 * n, None
            return None

        def vector():
            s = todo["x_low"]
            if s < len(stages) and self.x_on_vector(s) and have(("x_high", s)):
                return ("x_low", s), self.tiles_of(stages[s][0]) * P / 0.96 + 70, None
            u = todo["product"]
            s = stage_now()
            for q in lows:
                if have(("w_high", q)) and (pieces[q][0] - 1 <= s or u + LOW_UNITS >= self.of_stage[s][-1]
                                            or pieces[q][0] < EAGER_PIECES):
                    return ("w_low", q), (pieces[q][2] - pieces[q][1]) * D / 0.96 + 70, None
            ready = [f for f in finishes if have(("product", f)) and (
                units[f].how == "vector" or have(("sum", f, 1 if units[f].how == "tensor" else 0)))]
            left = {"vector": 1, "tensor": FOLDED / D}

            def finish(f):
                return ("finish", f), cols(f) * left.get(units[f].how, 0.5 ** units[f].halvings) / 0.96 + 70, None
            if ready and (lag(ready[0]) > LAG["vector"] or units[ready[0]].how == "tensor"):
                return finish(ready[0])
            if u < len(units) and have(("unit", u)) and summed(u - PRODUCT_SLOTS) and \
                    have(*[("gather", units[u].p, f) for f in range(units[u].m)]):
                return ("product", u), cols(u) / 0.96 + 70, None
            if ready:
                return finish(ready[0])
            for t in outs:
                if have(("mlp", t)) and busy["scalar"] > now + 600:
                    return ("mlp_out", t), 600, None
            return None

        def cold(stage):
            return 2 if stage[1] <= SLOW_STAGES[stage[0]] else 1

        def unit_cost(u):
            unit = units[u]
            banks = unit.tiles * -(-(unit.i1 - unit.i0) * D // BANK)
            return max(cols(u) * 0.842, banks * 108) * cold((unit.p, unit.m))

        def tensor():
            s = todo["transpose"]
            if s < len(stages) and have(("twin", s)) and turn_free() and units_done(s - X_SLOTS) \
                    and stage_now() >= s - X_SLOTS:
                return ("transpose", s), 110 * NB * cold(stages[s]), 110 * NB * cold(stages[s]) + 100
            s = todo["x_cut"] = max(todo["x_cut"], VECTOR_SPLITS)
            if s < len(stages) and have(("x_high", s)):
                return ("x_cut", s), 54 * self.tiles_of(stages[s][0]), 54 * self.tiles_of(stages[s][0]) + 200
            u = todo["unit"]
            unit_ok = False
            if u < len(units):
                s = self.stage_of[u]
                p, m = stages[s]
                operands = [("w_low", q) for q in self.pieces_of(m)] if p == 0 else [("fetch", s)]
                unit_ok = turn_free() and have(("x_low", s), *operands)
            folds = open_fold or [f for f in sums["tensor"] if have(("product", f))][:1]
            fold_ok = folds and (open_fold or len(self.folds) < 2 or have(("finish", self.folds[-2])))
            ahead = u - todo["product"]
            if fold_ok and (not unit_ok or ahead >= UNITS_AHEAD or lag(folds[0]) > LAG["tensor"]):
                half = 1 if open_fold else 0
                return ("sum", folds[0], half), cols(folds[0]) * 0.834 + 20, cols(folds[0]) * 0.834 + 200
            found = mlp(urgent=False)
            if found:
                return found
            if unit_ok and (ahead < UNITS_AHEAD or todo["mlp"] >= len(tasks)):
                return ("unit", u), unit_cost(u), unit_cost(u) + 100
            found = mlp(urgent=True)
            if found:
                return found
            if unit_ok:
                return ("unit", u), unit_cost(u), unit_cost(u) + 100
            return None

        def mlp(urgent):
            t = todo["mlp"]
            if t < len(tasks) and turn_free():
                task = tasks[t]
                due = (stage_now() - (len(PASSES) - 1) * (F - 1) - MLP_FROM) * MLP_PACE
                if not urgent and t >= min(due, self.late_tasks):
                    return None
                needs = {"zt": (), "h1_part": ("zt",), "h1": ("zt", "h1_part"), "h2": ("h1",), "y": ("h2",)}
                before = [("mlp_out", k) for k in range(t)
                          if tasks[k].p == task.p and tasks[k].kind in needs[task.kind]
                          and tasks[k].c0 <= task.c0 < tasks[k].c1]
                if task.kind == "zt":
                    mine = self.zt_needs(task)
                    ok = todo["product"] > max(mine) and all(summed(v) for v in mine) and have(("w1", 0))
                    before += [("mlp_out", k) for k in range(t) if tasks[k].p < task.p]
                else:
                    ok = True
                n = {"zt": 0.85, "h2": 6.8, "y": 3.4}.get(task.kind) or 1.69 * (task.k1 - task.k0 + (task.k0 > 0))
                n *= task.c1 - task.c0
                if ok and have(*before):
                    return ("mlp", t), n, n + 200
            return None

        def assign(u):
            unit = units[u]
            if unit.m <= DIRECT_SUMS[unit.p]:
                return "vector"
            spare = {"scalar": busy["scalar"] - now + work["scalar"],
                     "tensor": 2.6 * work["tensor"],
                     "gpsimd": max(busy["gpsimd"] - now, 0) + work["gpsimd"]}
            cost = {"scalar": 240 * unit.pairs, "tensor": 1.67 * cols(u), "gpsimd": 1.17 * cols(u)}
            if gathers and (gathers[0][0] == 0):
                spare["gpsimd"] = 1e9
            horizon = SUM_HORIZON[unit.p]
            late = {e: (max(spare[e], 0) + cost[e]) / horizon[e] for e in spare}
            best = min(late, key=late.get)
            if best == "gpsimd" and max(spare[best], 0) + 1.5 * cost[best] < TWO_HALVINGS:
                unit.halvings = 2
            return best if late[best] < 1 else "vector"

        pick = {"sync": sync, "gpsimd": gpsimd, "scalar": scalar, "vector": vector, "tensor": tensor}
        events = []
        while True:
            for e in self.ENGINES:
                if busy[e] > now:
                    continue
                found = pick[e]()
                if found is None:
                    continue
                step, cost, latency = found
                busy[e] = now + cost
                ready = now + (latency or cost) + self.SIGNAL
                done[step] = ready
                events += [busy[e], ready]
                self.order[e].append(step)
                kind, n = step[:2]
                if kind in todo:
                    todo[kind] += 1
                if kind in ("unit", "transpose", "mlp"):
                    self.turns.append((kind, n))
                if kind == "w_high":
                    lows.append(n)
                elif kind == "w_low":
                    lows.remove(n)
                    self.low_by[n] = e
                elif kind == "mlp":
                    outs.append(n)
                elif kind == "mlp_out":
                    outs.remove(n)
                    self.out_by[n] = e
                elif kind == "gather":
                    gathers.remove(step[1:])
                    if not gathers or gathers[0][:2] != step[1:3]:
                        done[step[:3]] = ready
                elif kind == "w1":
                    late_loads.clear()
                elif kind == "product":
                    how = units[n].how = assign(n)
                    if how != "scalar":
                        finishes.append(n)
                    if how != "vector":
                        sums[how].append(n)
                        work[how] += {"scalar": 240 * units[n].pairs, "tensor": 1.67 * cols(n),
                                      "gpsimd": halving(n)}[how]
                elif kind == "finish":
                    finishes.remove(n)
                elif kind == "sum":
                    how = units[n].how
                    work[how] -= cost
                    if how == "tensor" and step[2] == 0:
                        open_fold.append(n)
                        self.folds.append(n)
                    elif how == "scalar" and step[2]:
                        summing[0] = step[2]
                    else:
                        summing.clear() if how == "scalar" else None
                        open_fold.clear() if how == "tensor" else None
                        sums[how].remove(n)
            events = sorted({t for t in events if t > now})
            if not events:
                break
            now = events[0]
        self.end = now
        self.done = done
        assert todo["mlp"] == len(tasks) and not outs, "the rehearsal got stuck"


def build(nc, tables, ids, dense, weights, eye, w1, b1, w2, b2, w3, scratch, out):
    B, F = ids.shape
    D = tables[0].shape[1]
    TILES = B // P
    NB = TILES // HALVES
    WIDTH = NB * P
    PAIRS = F * (F - 1) // 2
    H1, H2 = w2.shape
    K1 = w1.shape[0]
    KT = -(-K1 // P)
    N1, N2 = H1 // P, H2 // P
    assert WIDTH == BANK
    plan = Plan(F, D, B, KT, N1, N2)
    units, pieces, of_stage, stages, tasks = plan.units, plan.pieces, plan.of_stage, plan.stages, plan.tasks
    base = [m * (m - 1) // 2 for m in range(F + 1)]

    with ExitStack() as ctx:
        def sb(name, shape, dt=F32):
            return ctx.enter_context(nc.sbuf_tensor(name, shape, dt))

        def ps(name, shape):
            return ctx.enter_context(nc.psum_tensor(name, shape, F32))

        def sem(name):
            return ctx.enter_context(nc.semaphore(name))

        idx = sb("idx", [P, TILES, F], I32)
        emb = sb("emb", [P, TILES, F * D])
        ident = sb("ident", [P, P])
        minus_ident = sb("minus_ident", [P, P], F32R)
        raw = sb("raw", [P, RAW_SLOTS, PIECE_PAIRS * D])
        wsplit = sb("wsplit", [P, 2 * (F - 1) * D], F32R)
        twin = sb("twin", [P, X_SLOTS, NB, 2, D])
        xsplit = sb("xsplit", [P, X_SLOTS, 2, WIDTH], F32R)
        prod = sb("prod", [P, PRODUCT_SLOTS, TURN_BANKS * BANK])
        z = sb("z", [P, TILES, K1])
        w3_sb = sb("w3_sb", [P, N2])
        b1_sb = sb("b1_sb", [P, N1])
        b2_sb = sb("b2_sb", [P, N2])
        assert N1 * H2 + B <= RAW_SLOTS * PIECE_PAIRS * D
        spare = raw.rearrange("p s c -> p (s c)")
        w2_sb = spare[:, 0:N1 * H2].rearrange("p (k n) -> p k n", k=N1)
        y_sb = spare[0:1, N1 * H2:N1 * H2 + B]
        free = emb[:, 0:NB, :].rearrange("p t c -> p (t c)")
        at = [0, KT * H1, KT * (H1 + WIDTH), KT * (H1 + WIDTH) + N1 * WIDTH,
              KT * (H1 + WIDTH) + (N1 + N2) * WIDTH]
        assert at[-1] <= NB * F * D
        w1_sb = free[:, at[0]:at[1]].rearrange("p (k n) -> p k n", k=KT)
        zt = free[:, at[1]:at[2]].rearrange("p (k b) -> p k b", k=KT)
        h1t = free[:, at[2]:at[3]].rearrange("p (k b) -> p k b", k=N1)
        h2t = free[:, at[3]:at[4]].rearrange("p (k b) -> p k b", k=N2)

        uacc = ps("uacc", [P, TURN_SLOTS, TURN_BANKS, BANK])
        fold = ps("fold", [P, 2, BANK])

        idx_loaded = sem("idx_loaded")
        ident_loaded = sem("ident_loaded")
        mlp_loaded = sem("mlp_loaded")
        gathered = [[sem(f"gathered{p}_{m}") for m in range(F)] for p in range(len(PASSES))]
        raw_loaded = [sem(f"raw_loaded{s}") for s in range(RAW_SLOTS)]
        twin_copied = [sem(f"twin_copied{s}") for s in range(X_SLOTS)]
        w_stored = [sem(f"w_stored{s}") for s in range(W_SEMAPHORES)]
        w_fetched = [sem(f"w_fetched{s}") for s in range(W_SEMAPHORES)]
        w_high_done = sem("w_high_done")
        w_low_by = {"vector": sem("w_low_by_vector"), "gpsimd": sem("w_low_by_gpsimd")}
        x_transposed = sem("x_transposed")
        minus_ready = sem("minus_ready")
        x_high_done = sem("x_high_done")
        x_cut = sem("x_cut")
        x_low_done = sem("x_low_done")
        u_ready = sem("u_ready")
        prod_ready = sem("prod_ready")
        halved = sem("halved")
        folded = sem("folded")
        z_by_vector = sem("z_by_vector")
        z_by_scalar = sem("z_by_scalar")
        mlp_acc = sem("mlp_acc")
        mlp_out_by = {"scalar": sem("mlp_out_by_scalar"), "vector": sem("mlp_out_by_vector")}
        out_stored = sem("out_stored")

        def count(steps):
            return {step[1]: k + 1 for k, step in enumerate(steps)}

        order = plan.order
        finish_count = count([step for step in order["vector"] if step[0] == "finish"])
        sum_count, low_count, out_count = {}, {}, {}
        for e in ("gpsimd", "scalar", "vector", "tensor"):
            sum_count |= count([step for step in order[e] if step[0] == "sum" and step[2] == (e == "tensor")])
            low_count |= count([step for step in order[e] if step[0] == "w_low"])
            out_count |= count([step for step in order[e] if step[0] == "mlp_out"])
        halved_count, halvings = {}, 0
        for step in order["gpsimd"]:
            if step[0] == "sum":
                halvings += units[step[1]].halvings
                halved_count[step[1]] = halvings
        turns = plan.turns
        turn_of = {turn: t for t, turn in enumerate(turns)}
        folds = plan.folds

        def wait_low(eng, q):
            eng.wait_ge(w_low_by[plan.low_by[q]], low_count[q])

        def wait_lows(eng, m):
            for q in plan.pieces_of(m):
                wait_low(eng, q)

        def wait_stored(eng, m):
            eng.wait_ge(w_stored[m % W_SEMAPHORES], 16 * len(range(m, 0, -W_SEMAPHORES)))

        def w_of(m, a, b):
            return slice((plan.w_at(m) + a) * D, (plan.w_at(m) + b) * D)

        def wait_task(eng, t):
            eng.wait_ge(mlp_out_by[plan.out_by[t]], out_count[t])

        def wait_summed(eng, u):
            if units[u].how == "scalar":
                eng.wait_ge(z_by_scalar, sum_count[u])
            else:
                eng.wait_ge(z_by_vector, finish_count[u])

        def wait_z(eng, task):
            mine = plan.zt_needs(task)
            eng.wait_ge(z_by_vector, max(finish_count[u] for u in mine if u in finish_count))
            eng.wait_ge(z_by_scalar, max(sum_count[u] for u in mine if units[u].how == "scalar"))

        def z_of(unit):
            c = base[unit.m] + unit.i0
            return z[:, unit.tile:unit.tile + unit.tiles, c:c + unit.i1 - unit.i0]

        def product_of(u):
            return prod[:, u % PRODUCT_SLOTS, 0:units[u].pairs * D]

        def acc(kind, n):
            return uacc[:, turn_of[kind, n] % TURN_SLOTS, :, :]

        def split_low(eng, q):
            m, a, b = pieces[q]
            eng.wait_ge(w_high_done, q + 1)
            w = wsplit[0:D, w_of(m, a, b)]
            eng.tensor_tensor(w, raw[0:D, q % RAW_SLOTS, 0:(b - a) * D], w.bitcast(F32),
                              ALU.subtract).then_inc(w_low_by[plan.low_by[q]], 1)

        block = ctx.enter_context(nc.Block())

        @block.sync
        def _(sp):
            sp.dma_start(idx[:, :, :], ids.rearrange("(t p) f -> p t f", p=P)).then_inc(idx_loaded, 16)
            sp.dma_start(ident[:, :], eye).then_inc(ident_loaded, 16)
            for kind, n, *_ in order["sync"]:
                if kind == "load":
                    m, a, b = pieces[n]
                    if n >= RAW_SLOTS:
                        wait_low(sp, n - RAW_SLOTS)
                    sp.dma_start(raw[:, n % RAW_SLOTS, 0:(b - a) * D],
                                 weights[:, (base[m] + a) * D:(base[m] + b) * D]
                                 ).then_inc(raw_loaded[n % RAW_SLOTS], 16)
                elif kind == "twin":
                    p, m = stages[n]
                    tiles = slice(*PASSES[p])
                    sp.wait_ge(gathered[p][m], 16 * plan.tiles_of(p))
                    if n >= X_SLOTS:
                        sp.wait_ge(x_transposed, n - X_SLOTS + 1)
                    for k in range(2):
                        sp.dma_start(twin[:, n % X_SLOTS, 0:plan.tiles_of(p), k, :], emb[:, tiles, m * D:(m + 1) * D]
                                     ).then_inc(twin_copied[n % X_SLOTS], 16)
                elif kind == "store":
                    wait_lows(sp, n)
                    sp.dma_start(scratch[:, base[n] * D:base[n + 1] * D], wsplit[:, w_of(n, 0, n)].bitcast(F32)
                                 ).then_inc(w_stored[n % W_SEMAPHORES], 16)
                elif kind == "fetch":
                    p, m = stages[n]
                    if n < 2 * (F - 1):
                        wait_stored(sp, m)
                    for k in plan.overwritten(n):
                        if k < F - 1:
                            wait_stored(sp, k + 1)
                    sp.wait_ge(u_ready, of_stage[plan.overwritten(n)[0]][-1] + 1)
                    sp.dma_start(wsplit[:, w_of(m, 0, m)].bitcast(F32), scratch[:, base[m] * D:base[m + 1] * D]
                                 ).then_inc(w_fetched[n % W_SEMAPHORES], 16)
                elif kind == "w1":
                    wait_lows(sp, F - 1)
                    last = of_stage[plan.first_half * (F - 1) - 1][-1]
                    sp.wait_ge(prod_ready, last + 1)
                    sp.dma_start(z[:, :, PAIRS:K1], dense.rearrange("(t p) f -> p t f", p=P)
                                 ).then_inc(mlp_loaded, 16)
                    sp.dma_start(w2_sb[:, :, :], w2.rearrange("(k p) n -> p k n", p=P)).then_inc(mlp_loaded, 16)
                    sp.dma_start(w3_sb[:, :], w3).then_inc(mlp_loaded, 16)
                    sp.dma_start(b1_sb[:, :], b1).then_inc(mlp_loaded, 16)
                    sp.dma_start(b2_sb[:, :], b2).then_inc(mlp_loaded, 16)
                    full = K1 // P
                    sp.dma_start(w1_sb[:, 0:full, :], w1[0:full * P, :].rearrange("(k p) n -> p k n", p=P)
                                 ).then_inc(mlp_loaded, 16)
                    sp.dma_start(w1_sb[0:K1 - full * P, full, :], w1[full * P:K1, :]).then_inc(mlp_loaded, 16)
            for t, task in enumerate(tasks):
                if task.kind == "y":
                    wait_task(sp, t)
            sp.dma_start(out.rearrange("b o -> o b"), y_sb[:, :]).then_inc(out_stored, 16)
            sp.wait_ge(out_stored, 16)

        @block.gpsimd
        def _(pool):
            pool.wait_ge(idx_loaded, 16)
            for kind, n, *rest in order["gpsimd"]:
                if kind == "gather":
                    m, t = rest
                    pool.indirect_dma_start(
                        emb[:, t, m * D:(m + 1) * D], None, tables[m][:, :],
                        bass.IndirectOffsetOnAxis(ap=idx[:, t, m:m + 1], axis=0)).then_inc(gathered[n][m], 16)
                elif kind == "w_low":
                    split_low(pool, n)
                elif kind == "sum":
                    v = product_of(n).rearrange("p (j d) -> p j d", d=D)
                    pool.wait_ge(prod_ready, n + 1)
                    for k in range(1, units[n].halvings + 1):
                        w = D >> k
                        if k > 1:
                            pool.wait_ge(halved, halved_count[n] - units[n].halvings + k - 1)
                        pool.tensor_tensor(v[:, :, 0:w], v[:, :, 0:w], v[:, :, w:2 * w], ALU.add).then_inc(halved, 1)

        @block.scalar
        def _(act):
            act.wait_ge(ident_loaded, 16)
            act.activation(minus_ident[:, :], ident[:, :], ACT.Copy, scale=-1.0).then_inc(minus_ready, 1)
            for kind, n, *rest in order["scalar"]:
                if kind == "w_high":
                    m, a, b = pieces[n]
                    act.wait_ge(raw_loaded[n % RAW_SLOTS], 16 * (n // RAW_SLOTS + 1))
                    old = plan.overwritten(m - 1)
                    if old:
                        act.wait_ge(u_ready, of_stage[old[0]][-1] + 1)
                    for k in old:
                        wait_stored(act, k + 1)
                    act.activation(wsplit[:, w_of(m, a, b)], raw[:, n % RAW_SLOTS, 0:(b - a) * D],
                                   ACT.Copy).then_inc(w_high_done, 1)
                elif kind == "x_high":
                    act.wait_ge(x_transposed, n + 1)
                    if n >= X_SLOTS:
                        act.wait_ge(u_ready, of_stage[n - X_SLOTS][-1] + 1)
                    rows = plan.tiles_of(stages[n][0]) * P
                    act.activation(xsplit[:, n % X_SLOTS, 0, 0:rows], acc("transpose", n)[:, 0, 0:rows],
                                   ACT.Copy).then_inc(x_high_done, 1)
                elif kind == "x_low":
                    act.wait_ge(x_cut, n + 1 - VECTOR_SPLITS)
                    rows = plan.tiles_of(stages[n][0]) * P
                    act.activation(xsplit[:, n % X_SLOTS, 1, 0:rows], acc("transpose", n)[:, 0, 0:rows],
                                   ACT.Copy).then_inc(x_low_done, 1)
                elif kind == "sum":
                    unit = units[n]
                    act.wait_ge(prod_ready, n + 1)
                    zv, pv, stop, each = z_of(unit), product_of(n), unit.pairs - rest[0], unit.i1 - unit.i0
                    for j in range((stop - 1) // SCALAR_PAIRS * SCALAR_PAIRS, stop):
                        last = act.activation(pv[:, j * D:(j + 1) * D], pv[:, j * D:(j + 1) * D], ACT.Copy,
                                              accum_out=zv[:, j // each, j % each:j % each + 1])
                    if rest[0] == 0:
                        last.then_inc(z_by_scalar, 1)
                elif kind == "mlp_out":
                    task = tasks[n]
                    act.wait_ge(mlp_acc, n + 1)
                    act.wait_ge(mlp_loaded, 7 * 16)
                    cols = slice(task.c0, task.c1)
                    rows = min(P, K1 - task.n * P)
                    src = acc("mlp", n)[:, 0, 0:task.c1 - task.c0]
                    if task.kind == "zt":
                        ins = act.activation(zt[0:rows, task.n, cols], src[0:rows, :], ACT.Copy)
                    elif task.kind == "h1_part":
                        ins = act.activation(h1t[:, task.n, cols], src, ACT.Copy)
                    elif task.kind == "h1":
                        ins = act.activation(h1t[:, task.n, cols], src, ACT.Relu, bias=b1_sb[:, task.n:task.n + 1])
                    elif task.kind == "h2":
                        ins = act.activation(h2t[:, task.n, cols], src, ACT.Relu, bias=b2_sb[:, task.n:task.n + 1])
                    else:
                        y = y_sb[0:1, task.p * WIDTH + task.c0:task.p * WIDTH + task.c1]
                        ins = act.activation(y, src[0:1, :], ACT.Copy)
                    ins.then_inc(mlp_out_by["scalar"], 1)

        @block.vector
        def _(dve):
            seen = [0] * len(PASSES)
            for kind, n, *rest in order["vector"]:
                if kind == "w_low":
                    split_low(dve, n)
                elif kind == "x_low":
                    dve.wait_ge(x_high_done, n + 1)
                    rows = plan.tiles_of(stages[n][0]) * P
                    dve.tensor_tensor(xsplit[:, n % X_SLOTS, 1, 0:rows], acc("transpose", n)[:, 0, 0:rows],
                                      xsplit[:, n % X_SLOTS, 0, 0:rows].bitcast(F32), ALU.subtract).then_inc(x_low_done, 1)
                elif kind == "product":
                    unit = units[n]
                    while seen[unit.p] < unit.m:
                        dve.wait_ge(gathered[unit.p][seen[unit.p]], 16 * plan.tiles_of(unit.p))
                        seen[unit.p] += 1
                    dve.wait_ge(u_ready, n + 1)
                    if n >= PRODUCT_SLOTS:
                        wait_summed(dve, n - PRODUCT_SLOTS)
                    width = (unit.i1 - unit.i0) * D
                    e = emb[:, unit.tile:unit.tile + unit.tiles, unit.i0 * D:unit.i1 * D]
                    if unit.tiles == 1:
                        u_in = acc("unit", n).rearrange("p c n -> p (c n)")[:, 0:width]
                        dve.tensor_tensor(product_of(n), u_in, e[:, 0, :], ALU.mult).then_inc(prod_ready, 1)
                    else:
                        dve.tensor_tensor(product_of(n).rearrange("p (t c) -> p t c", t=unit.tiles),
                                          acc("unit", n)[:, 0:unit.tiles, 0:width], e,
                                          ALU.mult).then_inc(prod_ready, 1)
                elif kind == "finish":
                    unit = units[n]
                    if unit.how == "tensor":
                        dve.wait_ge(folded, sum_count[n])
                        v = fold[:, (sum_count[n] - 1) % 2, 0:unit.pairs * FOLDED].rearrange(
                            "p (t j d) -> p t j d", t=unit.tiles, d=FOLDED)
                    else:
                        v = product_of(n).rearrange("p (t j d) -> p t j d", t=unit.tiles, d=D)
                        if unit.how == "gpsimd":
                            dve.wait_ge(halved, halved_count[n])
                            v = v[:, :, :, 0:D >> unit.halvings]
                        else:
                            dve.wait_ge(prod_ready, n + 1)
                    dve.tensor_reduce(z_of(unit), v, AX.X, ALU.add).then_inc(z_by_vector, 1)
                elif kind == "mlp_out":
                    task = tasks[n]
                    dve.wait_ge(mlp_acc, n + 1)
                    dve.wait_ge(mlp_loaded, 7 * 16)
                    cols = slice(task.c0, task.c1)
                    rows = min(P, K1 - task.n * P)
                    src = acc("mlp", n)[:, 0, 0:task.c1 - task.c0]
                    if task.kind == "zt":
                        ins = dve.tensor_copy(zt[0:rows, task.n, cols], src[0:rows, :])
                    elif task.kind == "h1_part":
                        ins = dve.tensor_copy(h1t[:, task.n, cols], src)
                    elif task.kind == "h1":
                        ins = dve.tensor_scalar(h1t[:, task.n, cols], src, b1_sb[:, task.n:task.n + 1], 0.0,
                                                ALU.add, ALU.max)
                    elif task.kind == "h2":
                        ins = dve.tensor_scalar(h2t[:, task.n, cols], src, b2_sb[:, task.n:task.n + 1], 0.0,
                                                ALU.add, ALU.max)
                    else:
                        y = y_sb[0:1, task.p * WIDTH + task.c0:task.p * WIDTH + task.c1]
                        ins = dve.tensor_copy(y, src[0:1, :])
                    ins.then_inc(mlp_out_by["vector"], 1)

        @block.tensor
        def _(pe):
            pe.wait_ge(ident_loaded, 16)

            def take_turn(kind, n):
                t = turn_of[kind, n] - TURN_SLOTS
                if t >= 0:
                    kind, n = turns[t]
                    if kind == "unit":
                        pe.wait_ge(prod_ready, n + 1)
                    elif kind == "transpose":
                        pe.wait_ge(x_low_done, n + 1)
                    else:
                        wait_task(pe, n)

            def wait_operand(p, kind, col, t):
                for k, task in enumerate(tasks[:t]):
                    if task.p == p and task.kind == kind and task.c0 <= col < task.c1:
                        wait_task(pe, k)

            for kind, n, *rest in order["tensor"]:
                if kind == "transpose":
                    pe.wait_ge(twin_copied[n % X_SLOTS], 32 * (n // X_SLOTS + 1))
                    take_turn(kind, n)
                    tiles = plan.tiles_of(stages[n][0])
                    for t in range(tiles):
                        last = pe.matmul(acc(kind, n)[:, 0, t * P:(t + 1) * P],
                                         twin[:, n % X_SLOTS, t, :, :].rearrange("p k d -> p (k d)"), ident[:, :],
                                         start=(t == 0), stop=(t == tiles - 1), is_transpose=True)
                    last.then_inc(x_transposed, 1)
                elif kind == "x_cut":
                    pe.wait_ge(minus_ready, 1)
                    pe.wait_ge(x_high_done, n + 1)
                    rows = plan.tiles_of(stages[n][0]) * P
                    pe.matmul(acc("transpose", n)[:, 0, 0:rows], minus_ident[:, :], xsplit[:, n % X_SLOTS, 0, 0:rows],
                              start=False, stop=True, skip_group_check=True).then_inc(x_cut, 1)
                elif kind == "unit":
                    unit = units[n]
                    s = unit.p * (F - 1) + unit.m - 1
                    if n == of_stage[s][0]:
                        pe.wait_ge(x_low_done, s + 1)
                        if unit.p == 0:
                            wait_lows(pe, unit.m)
                        else:
                            before = len(range(s % W_SEMAPHORES, F - 1, W_SEMAPHORES))
                            pe.wait_ge(w_fetched[s % W_SEMAPHORES], 16 * (s // W_SEMAPHORES + 1 - before))
                    take_turn(kind, n)
                    width = (unit.i1 - unit.i0) * D
                    w0 = w_of(unit.m, unit.i0, unit.i1).start
                    for t in range(unit.tiles):
                        b0 = (unit.tile + t - PASSES[unit.p][0]) * P
                        for part in range(2):
                            for c in range(0, width, BANK):
                                w = min(BANK, width - c)
                                last = pe.matmul(acc(kind, n)[:, t + c // BANK, 0:w],
                                                 xsplit[:, s % X_SLOTS, part, b0:b0 + P],
                                                 wsplit[:, w0 + c:w0 + c + w],
                                                 start=(part == 0), stop=(part == 1))
                    last.then_inc(u_ready, 1)
                elif kind == "sum":
                    half = rest[0]
                    k = folds.index(n)
                    if half == 0:
                        pe.wait_ge(prod_ready, n + 1)
                        if k >= 2:
                            pe.wait_ge(z_by_vector, finish_count[folds[k - 2]])
                    v = product_of(n).rearrange("p (j d) -> p j d", d=D)
                    dst = fold[:, k % 2, 0:units[n].pairs * FOLDED].rearrange("p (j d) -> p j d", d=FOLDED)
                    parts = D // FOLDED
                    for o in range(half * parts // 2, (half + 1) * parts // 2):
                        last = pe.matmul(dst, ident[:, :], v[:, :, o * FOLDED:(o + 1) * FOLDED],
                                         start=(o == 0), stop=(o == parts - 1))
                    if half == 1:
                        last.then_inc(folded, 1)
                elif kind == "mlp":
                    task = tasks[n]
                    if task.kind == "zt":
                        wait_z(pe, task)
                        pe.wait_ge(mlp_loaded, 7 * 16)
                    if task.kind == "zt" and task.n == 0 and task.p:
                        for k in range(n):
                            if tasks[k].kind == "y":
                                wait_task(pe, k)
                    take_turn(kind, n)
                    dst = acc(kind, n)[:, 0, 0:task.c1 - task.c0]
                    cols = slice(task.c0, task.c1)
                    if task.kind == "zt":
                        rows = min(P, K1 - task.n * P)
                        for t in range(task.c0 // P, task.c1 // P):
                            last = pe.transpose(dst[0:rows, t * P - task.c0:(t + 1) * P - task.c0],
                                                z[:, task.p * NB + t, task.n * P:task.n * P + rows], ident[:, :])
                    elif task.kind in ("h1", "h1_part"):
                        if task.k0:
                            wait_operand(task.p, "h1_part", task.c0, n)
                            pe.matmul(dst, ident[:, :], h1t[:, task.n, cols], start=True, stop=False)
                        wait_operand(task.p, "zt", task.c0, n)
                        for k in range(task.k0, task.k1):
                            rows = min(P, K1 - k * P)
                            last = pe.matmul(dst, w1_sb[0:rows, k, task.n * P:(task.n + 1) * P], zt[0:rows, k, cols],
                                             start=(k == 0), stop=(k == task.k1 - 1))
                    elif task.kind == "h2":
                        wait_operand(task.p, "h1", task.c0, n)
                        for k in range(N1):
                            last = pe.matmul(dst, w2_sb[:, k, task.n * P:(task.n + 1) * P], h1t[:, k, cols],
                                             start=(k == 0), stop=(k == N1 - 1))
                    else:
                        wait_operand(task.p, "h2", task.c0, n)
                        for k in range(N2):
                            last = pe.matmul(dst[0:1, :], w3_sb[:, k:k + 1], h2t[:, k, cols],
                                             start=(k == 0), stop=(k == N2 - 1))
                    last.then_inc(mlp_acc, 1)


def kernel(**inputs):
    import numpy as np
    import concourse.bacc as bacc
    from concourse import mybir as mb
    from concourse.bass_utils import run_bass_kernel_spmd as run

    B, F = inputs["ids"].shape
    i_of, j_of = np.triu_indices(F, k=1)
    order = np.lexsort((i_of, j_of))
    W = np.asarray(inputs["L0_rec_W"])
    D = W.shape[1]
    w1 = np.asarray(inputs["W_top1"])
    pairs = len(order)
    arrays = {f"tbl_{f}": np.asarray(inputs[f"tbl_{f}"]) for f in range(F)}
    arrays |= {
        "ids": np.asarray(inputs["ids"]),
        "dense": np.asarray(inputs["dense_ctx"]),
        "weights": np.concatenate([W[order].transpose(2, 0, 1).reshape(D, pairs * D)] * 2, axis=0),
        "eye": np.eye(P, dtype=np.float32),
        "w1": np.concatenate([w1[order], w1[pairs:]], axis=0),
        "b1": np.asarray(inputs["b_top1"]).reshape(-1, P).T,
        "w2": np.asarray(inputs["W_top2"]),
        "b2": np.asarray(inputs["b_top2"]).reshape(-1, P).T,
        "w3": np.asarray(inputs["W_top3"]).reshape(-1, P).T,
    }
    nc = bacc.Bacc("TRN2", target_bir_lowering=False, num_devices=1)
    arrays = {f"in_{k}": np.ascontiguousarray(a) for k, a in arrays.items()}
    ap = {k: nc.dram_tensor(k, a.shape, mb.dt.from_np(a.dtype), kind="ExternalInput").ap()
          for k, a in arrays.items()}
    out = nc.dram_tensor("out_y", (B, 1), mb.dt.from_np(np.dtype("float32")), kind="ExternalOutput").ap()
    scratch = nc.dram_tensor("split_weights", (P, pairs * D), mb.dt.float32, kind="Internal").ap()
    build(nc, [ap[f"in_tbl_{f}"] for f in range(F)], ap["in_ids"], ap["in_dense"], ap["in_weights"], ap["in_eye"],
          ap["in_w1"], ap["in_b1"], ap["in_w2"], ap["in_b2"], ap["in_w3"], scratch, out)
    result = run(nc, [arrays], core_ids=[0])
    return result.results[0]["out_y"]
```
